# Optimizing a Trainium2 kernel written in Bass

```python
import numpy as np
import jax
import jax.numpy as jnp

def _softmax(x, axis=-1):
    return jax.nn.softmax(x, axis=axis)

def _gelu(x):
    return jax.nn.gelu(x, approximate=True)

def _silu(x):
    return jax.nn.silu(x)

def _sigmoid(x):
    return jax.nn.sigmoid(x)

def _layernorm(x, axis=-1, eps=1e-05):
    m = jnp.mean(x, axis=axis, keepdims=True)
    v = jnp.var(x, axis=axis, keepdims=True)
    return (x - m) / jnp.sqrt(v + eps)

def _scatter_add(tgt, idx, src, axis=0):
    return tgt.at[idx].add(src)

def _segment_sum(src, seg, n):
    return jax.ops.segment_sum(src, seg, n)
kernel_name = 'mk_conv_attn_hybrid_d2_conv_nchw512_r2_1d8b85'

def setup_inputs(seed: int=0):
    np.random.seed(seed)
    _w = jnp.asarray

    def _rec_inputs():
        import jax
        import jax.numpy as jnp
        _gk = jax.random.key(seed)
        x = -0.0002928 + 1 * jax.random.normal(jax.random.fold_in(_gk, 1), (8, 256, 32, 32), jnp.float32)
        return x
    x = _rec_inputs()

    def _L0_conv_setup():
        import jax, jax.numpy as jnp
        import numpy as np
        import math
        N_GROUPS = 32
        N_HEADS = 8
        EPS = 1e-05

        def _group_norm(x, w, b):
            B, C, L = x.shape
            xg = x.reshape(B, N_GROUPS, C // N_GROUPS, L)
            mean = jnp.mean(xg, axis=(2, 3), keepdims=True)
            var = jnp.var(xg, axis=(2, 3), keepdims=True)
            xn = ((xg - mean) * jax.lax.rsqrt(var + EPS)).reshape(B, C, L)
            return xn * w[None, :, None] + b[None, :, None]
        key = jax.random.key(seed)
        ks = jax.random.split(key, 6)
        B, C, Hs, Ws = (8, 256, 32, 32)
        x = jax.random.normal(ks[0], (B, C, Hs, Ws), dtype=jnp.float32)
        gn_w = jnp.ones((C,), dtype=jnp.float32)
        gn_b = jnp.zeros((C,), dtype=jnp.float32)
        w_qkv = jax.random.normal(ks[1], (3 * C, C), dtype=jnp.float32) * 0.02
        b_qkv = jax.random.normal(ks[2], (3 * C,), dtype=jnp.float32) * 0.02
        w_proj = jax.random.normal(ks[3], (C, C), dtype=jnp.float32) * 0.02
        b_proj = jax.random.normal(ks[4], (C,), dtype=jnp.float32) * 0.02
        return {'x': x, 'gn_w': gn_w, 'gn_b': gn_b, 'w_qkv': w_qkv, 'b_qkv': b_qkv, 'w_proj': w_proj, 'b_proj': b_proj}
    _L0_conv_all = _L0_conv_setup()
    _L0_conv_in = {k: v for k, v in _L0_conv_all.items() if k in ('gn_w', 'gn_b', 'w_qkv', 'b_qkv', 'w_proj', 'b_proj')}
    del _L0_conv_all

    def _L1_attn_setup():
        import jax, jax.numpy as jnp
        import numpy as np
        B, N, C, H = (128, 100, 256, 8)
        D = C // H
        BASE = 10000.0

        def _rope(x):
            d = x.shape[-1]
            inv_freq = 1.0 / BASE ** (jnp.arange(0, d, 2, dtype=jnp.float32) / d)
            t = jnp.arange(x.shape[1], dtype=jnp.float32)
            freqs = jnp.outer(t, inv_freq)
            emb = jnp.concatenate([freqs, freqs], axis=-1)
            cos = jnp.cos(emb)[None, :, None, :]
            sin = jnp.sin(emb)[None, :, None, :]
            x1, x2 = (x[..., :d // 2], x[..., d // 2:])
            return x * cos + jnp.concatenate([-x2, x1], axis=-1) * sin
        key = jax.random.key(seed)
        k0, k1, k2 = jax.random.split(key, 3)
        x = jax.random.normal(k0, (B, N, C), jnp.float32)
        Wqk = jax.random.normal(k1, (C, 2 * C), jnp.float32) * C ** (-0.5)
        bqk = jnp.zeros((2 * C,), jnp.float32)
        lepe_w = jax.random.normal(k2, (C, 1, 3), jnp.float32) * 0.3
        lepe_b = jnp.zeros((C,), jnp.float32)
        return {'x': x, 'Wqk': Wqk, 'bqk': bqk, 'lepe_w': lepe_w, 'lepe_b': lepe_b}
    _L1_attn_all = _L1_attn_setup()
    _L1_attn_in = {k: v for k, v in _L1_attn_all.items() if k in ('Wqk', 'bqk', 'lepe_w', 'lepe_b')}
    del _L1_attn_all

    def _L1_ffn_setup():
        import jax, jax.numpy as jnp
        import numpy as np

        def _haar_dwt2(x):
            a = x[:, ::2, ::2]
            b = x[:, ::2, 1::2]
            c = x[:, 1::2, ::2]
            d = x[:, 1::2, 1::2]
            ll = (a + b + c + d) * 0.5
            lh = (a + b - c - d) * 0.5
            hl = (a - b + c - d) * 0.5
            hh = (a - b - c + d) * 0.5
            return (ll, lh, hl, hh)

        def _haar_idwt2(ll, lh, hl, hh):
            a = (ll + lh + hl + hh) * 0.5
            b = (ll + lh - hl - hh) * 0.5
            c = (ll - lh + hl - hh) * 0.5
            d = (ll - lh - hl + hh) * 0.5
            B, H2, W2 = ll.shape
            out = jnp.zeros((B, 2 * H2, 2 * W2), ll.dtype)
            out = out.at[:, ::2, ::2].set(a)
            out = out.at[:, ::2, 1::2].set(b)
            out = out.at[:, 1::2, ::2].set(c)
            out = out.at[:, 1::2, 1::2].set(d)
            return out

        def _interp_linear_last(x, m):
            n = x.shape[-1]
            pos = jnp.linspace(0.0, 1.0, m, dtype=x.dtype) * (n - 1)
            i0 = jnp.clip(jnp.floor(pos).astype(jnp.int32), 0, n - 2)
            w = pos - i0.astype(x.dtype)
            return x[..., i0] * (1.0 - w) + x[..., i0 + 1] * w
        key = jax.random.key(seed)
        k0, k1, k2 = jax.random.split(key, 3)
        b, f, c, hidden = (64, 128, 256, 1024)
        x = jax.random.normal(k0, (b, f, c), dtype=jnp.float32)
        fc1_w = jax.random.normal(k1, (hidden, c), dtype=jnp.float32) * 0.02
        fc1_b = jnp.zeros((hidden,), dtype=jnp.float32)
        fc2_w = jax.random.normal(k2, (c // 2, hidden), dtype=jnp.float32) * 0.02
        fc2_b = jnp.zeros((c // 2,), dtype=jnp.float32)
        return {'x': x, 'fc1_w': fc1_w, 'fc1_b': fc1_b, 'fc2_w': fc2_w, 'fc2_b': fc2_b}
    _L1_ffn_all = _L1_ffn_setup()
    _L1_ffn_in = {k: v for k, v in _L1_ffn_all.items() if k in ('fc1_w', 'fc1_b', 'fc2_w', 'fc2_b')}
    del _L1_ffn_all
    return {'x': x, 'L0_conv_gn_w': _L0_conv_in['gn_w'], 'L0_conv_gn_b': _L0_conv_in['gn_b'], 'L0_conv_w_qkv': _L0_conv_in['w_qkv'], 'L0_conv_b_qkv': _L0_conv_in['b_qkv'], 'L0_conv_w_proj': _L0_conv_in['w_proj'], 'L0_conv_b_proj': _L0_conv_in['b_proj'], 'L1_attn_Wqk': _L1_attn_in['Wqk'], 'L1_attn_bqk': _L1_attn_in['bqk'], 'L1_attn_lepe_w': _L1_attn_in['lepe_w'], 'L1_attn_lepe_b': _L1_attn_in['lepe_b'], 'L1_ffn_fc1_w': _L1_ffn_in['fc1_w'], 'L1_ffn_fc1_b': _L1_ffn_in['fc1_b'], 'L1_ffn_fc2_w': _L1_ffn_in['fc2_w'], 'L1_ffn_fc2_b': _L1_ffn_in['fc2_b']}

def reference(x, L0_conv_gn_w, L0_conv_gn_b, L0_conv_w_qkv, L0_conv_b_qkv, L0_conv_w_proj, L0_conv_b_proj, L1_attn_Wqk, L1_attn_bqk, L1_attn_lepe_w, L1_attn_lepe_b, L1_ffn_fc1_w, L1_ffn_fc1_b, L1_ffn_fc2_w, L1_ffn_fc2_b):
    import jax
    import jax.numpy as jnp

    def _L0_conv_ref(x, gn_w, gn_b, w_qkv, b_qkv, w_proj, b_proj):
        import jax, jax.numpy as jnp
        import numpy as np
        import math
        N_GROUPS = 32
        N_HEADS = 8
        EPS = 1e-05

        def _group_norm(x, w, b):
            B, C, L = x.shape
            xg = x.reshape(B, N_GROUPS, C // N_GROUPS, L)
            mean = jnp.mean(xg, axis=(2, 3), keepdims=True)
            var = jnp.var(xg, axis=(2, 3), keepdims=True)
            xn = ((xg - mean) * jax.lax.rsqrt(var + EPS)).reshape(B, C, L)
            return xn * w[None, :, None] + b[None, :, None]
        B, C, Hs, Ws = x.shape
        L = Hs * Ws
        xf = x.reshape(B, C, L)
        xn = _group_norm(xf, gn_w, gn_b)
        qkv = jnp.einsum('oc,bcl->bol', w_qkv, xn) + b_qkv[None, :, None]
        ch = C // N_HEADS
        qkv = qkv.reshape(B * N_HEADS, 3 * ch, L)
        q, k, v = (qkv[:, :ch], qkv[:, ch:2 * ch], qkv[:, 2 * ch:])
        scale = 1.0 / math.sqrt(math.sqrt(ch))
        weight = jnp.einsum('bct,bcs->bts', q * scale, k * scale)
        weight = jax.nn.softmax(weight.astype(jnp.float32), axis=1).astype(weight.dtype)
        a = jnp.einsum('bts,bcs->bct', weight, v)
        a = a.reshape(B, C, L)
        h = jnp.einsum('oc,bcl->bol', w_proj, a) + b_proj[None, :, None]
        return (xf + h).reshape(B, C, Hs, Ws)

    def _L1_attn_ref(x, Wqk, bqk, lepe_w, lepe_b):
        import jax, jax.numpy as jnp
        import numpy as np
        B, N, C, H = (128, 100, 256, 8)
        D = C // H
        BASE = 10000.0

        def _rope(x):
            d = x.shape[-1]
            inv_freq = 1.0 / BASE ** (jnp.arange(0, d, 2, dtype=jnp.float32) / d)
            t = jnp.arange(x.shape[1], dtype=jnp.float32)
            freqs = jnp.outer(t, inv_freq)
            emb = jnp.concatenate([freqs, freqs], axis=-1)
            cos = jnp.cos(emb)[None, :, None, :]
            sin = jnp.sin(emb)[None, :, None, :]
            x1, x2 = (x[..., :d // 2], x[..., d // 2:])
            return x * cos + jnp.concatenate([-x2, x1], axis=-1) * sin
        b, n, c = x.shape
        h, d = (H, C // H)
        qk = x @ Wqk + bqk
        q = jax.nn.elu(qk[..., :c]) + 1.0
        k = jax.nn.elu(qk[..., c:]) + 1.0
        qh = q.reshape(b, n, h, d)
        kh = k.reshape(b, n, h, d)
        vh = x.reshape(b, n, h, d)
        q_r = _rope(qh).transpose(0, 2, 1, 3)
        k_r = _rope(kh).transpose(0, 2, 1, 3)
        qh = qh.transpose(0, 2, 1, 3)
        kh = kh.transpose(0, 2, 1, 3)
        vh = vh.transpose(0, 2, 1, 3)
        kmean = kh.mean(axis=2)
        z = 1.0 / (jnp.einsum('bhnd,bhd->bhn', qh, kmean) + 1e-06)
        scale = n ** (-0.5)
        kv = jnp.einsum('bhnd,bhne->bhde', k_r * scale, vh * scale)
        out = jnp.einsum('bhnd,bhde->bhne', q_r, kv) * z[..., None]
        out = out.transpose(0, 2, 1, 3).reshape(b, n, c)
        v_ncw = x.transpose(0, 2, 1)
        lepe = jax.lax.conv_general_dilated(v_ncw, lepe_w, window_strides=(1,), padding=[(1, 1)], feature_group_count=c, dimension_numbers=('NCH', 'OIH', 'NCH'))
        lepe = lepe + lepe_b[None, :, None]
        return out + lepe.transpose(0, 2, 1)

    def _L1_ffn_ref(x, fc1_w, fc1_b, fc2_w, fc2_b):
        import jax, jax.numpy as jnp
        import numpy as np

        def _haar_dwt2(x):
            a = x[:, ::2, ::2]
            b = x[:, ::2, 1::2]
            c = x[:, 1::2, ::2]
            d = x[:, 1::2, 1::2]
            ll = (a + b + c + d) * 0.5
            lh = (a + b - c - d) * 0.5
            hl = (a - b + c - d) * 0.5
            hh = (a - b - c + d) * 0.5
            return (ll, lh, hl, hh)

        def _haar_idwt2(ll, lh, hl, hh):
            a = (ll + lh + hl + hh) * 0.5
            b = (ll + lh - hl - hh) * 0.5
            c = (ll - lh + hl - hh) * 0.5
            d = (ll - lh - hl + hh) * 0.5
            B, H2, W2 = ll.shape
            out = jnp.zeros((B, 2 * H2, 2 * W2), ll.dtype)
            out = out.at[:, ::2, ::2].set(a)
            out = out.at[:, ::2, 1::2].set(b)
            out = out.at[:, 1::2, ::2].set(c)
            out = out.at[:, 1::2, 1::2].set(d)
            return out

        def _interp_linear_last(x, m):
            n = x.shape[-1]
            pos = jnp.linspace(0.0, 1.0, m, dtype=x.dtype) * (n - 1)
            i0 = jnp.clip(jnp.floor(pos).astype(jnp.int32), 0, n - 2)
            w = pos - i0.astype(x.dtype)
            return x[..., i0] * (1.0 - w) + x[..., i0 + 1] * w
        b, f, c = x.shape
        ll, lh, hl, hh = _haar_dwt2(x)
        ll_up = _interp_linear_last(ll, c)
        h = jax.nn.gelu(jnp.einsum('bfc,hc->bfh', ll_up, fc1_w) + fc1_b, approximate=False)
        ll_new = jnp.einsum('bfh,oh->bfo', h, fc2_w) + fc2_b
        return _haar_idwt2(ll_new, lh, hl, hh)

    def _gn(v, G=32, eps=1e-05):
        B_, C_, H_, W_ = v.shape
        g = v.reshape(B_, G, C_ // G, H_, W_)
        m = jnp.mean(g, axis=(2, 3, 4), keepdims=True)
        s = jnp.var(g, axis=(2, 3, 4), keepdims=True)
        return ((g - m) / jnp.sqrt(s + eps)).reshape(v.shape)

    def _ln_c(v, eps=1e-06):
        m = jnp.mean(v, axis=1, keepdims=True)
        s = jnp.var(v, axis=1, keepdims=True)
        return (v - m) / jnp.sqrt(s + eps)

    def _ln_t(v, eps=1e-05):
        m = jnp.mean(v, axis=-1, keepdims=True)
        s = jnp.var(v, axis=-1, keepdims=True)
        return (v - m) / jnp.sqrt(s + eps)

    def _to_tokens(v):
        B_, C_, H_, W_ = v.shape
        return v.reshape(B_, C_, H_ * W_).transpose(0, 2, 1)

    def _from_tokens(t, like):
        B_, C_, H_, W_ = like.shape
        return t.transpose(0, 2, 1).reshape(B_, C_, H_, W_)
    x = _L0_conv_ref(x, L0_conv_gn_w, L0_conv_gn_b, L0_conv_w_qkv, L0_conv_b_qkv, L0_conv_w_proj, L0_conv_b_proj)
    t = _to_tokens(x)
    t = t + _L1_attn_ref(_ln_t(t), L1_attn_Wqk, L1_attn_bqk, L1_attn_lepe_w, L1_attn_lepe_b)
    t = t + _L1_ffn_ref(_ln_t(t), L1_ffn_fc1_w, L1_ffn_fc1_b, L1_ffn_fc2_w, L1_ffn_fc2_b)
    x = _from_tokens(t, x)
    return x

_drawn_inputs = setup_inputs


def setup_inputs(seed=0):
    import zlib

    import numpy as np

    out = dict(_drawn_inputs(seed))
    spreads = {'L0_conv_gn_w': (1.0, 0.6),
     'L0_conv_gn_b': (0.0, 0.652),
     'L1_attn_bqk': (0.0, 2.0),
     'L1_attn_lepe_b': (0.0, 0.305),
     'L1_ffn_fc1_b': (0.0, 0.8),
     'L1_ffn_fc2_b': (0.0, 0.289)}
    factors = {'L0_conv_w_qkv': 4.471,
     'L0_conv_b_qkv': 7.305,
     'L0_conv_w_proj': 3.935,
     'L1_attn_Wqk': 28.754,
     'L0_conv_b_proj': 8.0,
     'L1_ffn_fc1_w': 4.923}
    for name, (base, spread) in spreads.items():
        noise = np.random.default_rng([zlib.crc32(name.encode()), seed]).standard_normal(out[name].shape)
        drawn = base * np.exp(spread * noise) if base else spread * noise
        out[name] = jnp.asarray(drawn.astype(out[name].dtype))
    for name, factor in factors.items():
        out[name] = (out[name] * factor).astype(out[name].dtype)
    return out
```

```python
from contextlib import ExitStack

import numpy as np

import concourse.bass as bass
from concourse import mybir

F32 = mybir.dt.float32
F32R = mybir.dt.float32r
ALU = mybir.AluOpType
ACT = mybir.ActivationFunctionType
AX_X = mybir.AxisListType.X

P = 128
B, C, L = 8, 256, 1024
NC = C // P
NG = 2
HG, D = 4, 32
NB = L // P
HALF = 512
HID = 1024
LL = C // 2
GN_SIZE = 8
UNITS = NG * NB * HG
PHASE = NB * HG
DMA = 16

CONSTS = {}
_at = 0
for _name, _width in (("ident", P), ("gn_mean", P), ("rot_t", P), ("rot", P), ("head_mask", P),
                      ("head_mean", HG), ("pair_rows", P // 2), ("spread", C), ("interp", NC * LL),
                      ("minus_half", 4), ("cos_tok", NB * D), ("sin_tok", NB * D),
                      ("cos_ch", L), ("sin_ch", L)):
    CONSTS[_name] = (_at, _at + _width)
    _at += _width
CONST_W = _at

PARAMS = {}
_at = 0
for _name, _width in (("bq", 2), ("bk", 2), ("bproj", 2), ("bqk", 4), ("lepe_w", 6), ("lepe_b", 2),
                      ("b1", 8), ("b2", 1), ("gn_w", 2), ("gn_b", 2), ("bv", C)):
    PARAMS[_name] = (_at, _at + _width)
    _at += _width
PARAM_W = _at

POST_AT = {
    4: [("proj", 0)], 5: [("proj", 1)], 6: [("proj", 2)], 7: [("proj", 3)],
    8: [("x1T", 0)], 9: [("x1T", 1)], 10: [("x1T", 2)], 11: [("x1T", 3)],
    12: [("lnT", 0)], 13: [("lnT", 1)], 14: [("lnT", 2)], 15: [("lnT", 3)],
    16: [("k", 0)], 17: [("k", 1)], 18: [("k", 2)], 19: [("k", 3)],
    20: [("kT", 0)], 21: [("kT", 1)], 22: [("kv", 0)], 24: [("kv2", 0), ("kT", 2)], 25: [("kT", 3)],
    26: [("kv", 1), ("q", 0)], 27: [("q", 1)], 28: [("kv2", 1), ("q", 2)], 29: [("q", 3)],
    31: [("den", 0)], 33: [("out", 0)], 34: [("out", 1)], 38: [("out", 2)], 39: [("out", 3)],
    40: [("uT", 0)], 41: [("uT", 1)], 42: [("uT", 2)], 43: [("uT", 3)],
    48: [("ll", 0)], 49: [("fc1", n) for n in range(8)], 50: [("fc2", 0)],
    51: [("rT", 0)], 52: [("rT", 1)], 53: [("rT", 2)], 54: [("rT", 3)],
    55: [("up", 0)], 56: [("up", 1)],
}
ELU_AT = {17: 0, 18: 1, 19: 2, 20: 3, 27: 4, 28: 5, 29: 6, 30: 7}
PRE1_AT = {13: [("pq1", 0)], 15: [("pq1", 1)], 22: [("pk1", 0)], 24: [("pk1", 1)],
           28: [("pv1", 0)], 30: [("pv1", 1)]}
PRE0_AT = {38: [("gn", 0)], 46: [("pq0", 0)], 47: [("pq0", 1)], 54: [("pk0", 0)], 56: [("pk0", 1)],
           58: [("pv0", 0)], 60: [("pv0", 1)]}
AHEAD = {"gn": 1, "pq0": 1, "pk0": 1, "pv0": 1, "pq1": 0, "pk1": 0, "pv1": 0}


def tiles_of(post, pre1, pre0):
    out = []
    for s in range(UNITS):
        for on, at in ((post, POST_AT), (pre1, PRE1_AT), (pre0, PRE0_AT)):
            if on:
                out += at.get(s, [])
    return out


STEADY = tiles_of(True, True, True)
BANK = {tile: n % 2 for n, tile in enumerate(STEADY)}
LISTS = {"prologue": [("w1", 0), ("w1", 1)] + [t for ts in PRE0_AT.values() for t in ts],
         "first": tiles_of(False, True, True), "steady": STEADY,
         "last": tiles_of(True, True, False), "epilogue": tiles_of(True, False, False)}
BEFORE = {"first": "prologue", "steady": "steady", "last": "steady", "epilogue": "last"}
BANK[("w1", 0)], BANK[("w1", 1)] = 0, 1


def tile_before(kind, tile):
    here = LISTS[kind]
    same = [t for t in here[:here.index(tile)] if BANK[t] == BANK[tile]]
    if same:
        return same[-1], 0
    if kind == "prologue":
        return None, 0
    return [t for t in LISTS[BEFORE[kind]] if BANK[t] == BANK[tile]][-1], 1


for _bank in (0, 1):
    _last = {k: [t for t in LISTS[k] if BANK[t] == _bank][-1] for k in ("prologue", "first", "steady")}
    assert len(set(_last.values())) == 1, _last


def build(nc, x, wqkv_t, wproj_t, wqk, fc1_t, fc2_t, params, consts, out):
    with ExitStack() as ctx:
        def sb(name, shape, dt=F32):
            return ctx.enter_context(nc.sbuf_tensor(name, shape, dt))

        def sem(name):
            return ctx.enter_context(nc.semaphore(name))

        x_v = x.rearrange("b (c p) h w -> b p c (h w)", p=P)
        out_v = out.rearrange("b (c p) h w -> b p c (h w)", p=P)

        w_qkv = sb("w_qkv", [P, NC, 3 * C])
        w_proj = sb("w_proj", [P, NC, C])
        w_qk = sb("w_qk", [P, NC, 2 * C])
        w1 = sb("w1", [P, HID])
        w2 = sb("w2", [P, HID // P, LL])
        par = sb("par", [P, PARAM_W])
        con = sb("con", [P, CONST_W])

        xg = sb("xg", [P, NC, L])
        gn_stats = sb("gn_stats", [P, NC, 2, 6])
        gn_mom = sb("gn_mom", [P, NC, 2])
        gn_sq = sb("gn_sq", [P, NC])
        gn_grp = sb("gn_grp", [P, NC, 2])
        gn_var = sb("gn_var", [P, NC])
        gn_rs = sb("gn_rs", [P, NC])
        gn_a = sb("gn_a", [P, NC])
        gn_ma = sb("gn_ma", [P, NC])
        gn_sh = sb("gn_sh", [P, NC])
        hi = sb("hi", [P, L], F32R)
        lo = sb("lo", [P, L], F32R)
        q_st = [sb(f"q_st{g}", [P, HG, L], F32R) for g in range(NG)]
        k_st = sb("k_st", [P, HG, L], F32R)
        v_tok = [sb(f"v_tok{g}", [P, NB, P]) for g in range(NG)]
        v_scaled = sb("v_scaled", [P, 2, P])
        probs = sb("probs", [P, 2, HG, L])
        negmax = sb("negmax", [P, 4])
        sums = sb("sums", [P, 2, HG])
        rsums = sb("rsums", [P, 2, HG])
        att = sb("att", [P, NG, L])

        x1 = sb("x1", [P, NC, L])
        tok = sb("tok", [P, NB, C])
        ln_ch = sb("ln_ch", [P, NC, L + 2])
        shared = sb("shared", [P, 2 * C // P * L])
        qk_ch = shared[:, 0:2 * L].rearrange("p (g n) -> p g n", g=NG)
        rot_tok = shared[:, 2 * L:4 * L].rearrange("p (r b c) -> p r b c", r=2, b=NB)
        rot_ch = shared[:, 2 * L:4 * L].rearrange("p (r n) -> p r n", r=2)
        hid = shared[:, :].rearrange("p (k m) -> p k m", k=HID // P)
        elu_x = sb("elu_x", [P, 2, HALF])
        csum = elu_x[:, :, :].rearrange("p a n -> p (a n)").rearrange("p (b c) -> p b c", b=NB)
        fc1_nat = probs[:, 0, 0:2, :]
        t2 = sb("t2", [P, NB, C])
        elu_e = t2[:, 0:4, :].rearrange("p (a n) c -> p a (n c)", a=2)
        band = sb("band", [P, HALF])
        wait_carrier = sb("wait_carrier", [P, 1])
        ln_st = sb("ln_st", [P, 2, 6])
        ln_mv = sb("ln_mv", [P, 4, 2, 2])
        ln_var = sb("ln_var", [P, 4, 2])
        ln_rs = sb("ln_rs", [P, 4, 2])
        ksum = sb("ksum", [P, 4])
        ksum_g = sb("ksum_g", [P, NG])
        kmean = sb("kmean", [P, NG, HG])
        kv_b = sb("kv_b", [P, NG, P])
        kv_c = sb("kv_c", [P, NG, P])
        kv_s = sb("kv_s", [P, NG, P])
        den = sb("den", [P, NB * NG * HG])
        zden = sb("zden", [P, NB, NG, HG])

        ps_s = [ctx.enter_context(nc.psum_tensor(f"ps_s{n}", [P, L], F32)) for n in range(2)]
        ps_o = ctx.enter_context(nc.psum_tensor("ps_o", [P, L], F32))
        work = [ctx.enter_context(nc.psum_tensor(f"work{n}", [P, HALF], F32)) for n in range(2)]

        def bank(tile):
            return work[BANK[tile]]

        def const(name):
            return con[:, CONSTS[name][0]:CONSTS[name][1]]

        def param(name, n=None):
            a, b = PARAMS[name]
            return par[:, a:b] if n is None else par[:, a + n:a + n + 1]

        weights_in = sem("weights_in")
        weights_ready = sem("weights_ready")
        edges_zero = sem("edges_zero")
        x_in = sem("x_in")
        xres_in = sem("xres_in")
        stored = sem("stored")
        gn_step = sem("gn_step")
        gn_rsqrt = sem("gn_rsqrt")
        gn_done = sem("gn_done")
        hi_done = sem("hi_done")
        lo_done = sem("lo_done")
        q_stacked = sem("q_stacked")
        k_stacked_a = sem("k_stacked_a")
        k_stacked_b = sem("k_stacked_b")
        v_done = sem("v_done")
        scores_ready = sem("scores_ready")
        max_ready = sem("max_ready")
        probs_ready = sem("probs_ready")
        rsums_ready = sem("rsums_ready")
        v_scaled_ready = sem("v_scaled_ready")
        pv_done = sem("pv_done")
        att_done = sem("att_done")
        made = {}
        for name in dict.fromkeys(t[0] for k in LISTS.values() for t in k):
            made[name] = sem("made_" + name)
        kv_half = sem("kv_half")
        x1_done = sem("x1_done")
        ln1_step = sem("ln1_step")
        ln1_rsqrt = sem("ln1_rsqrt")
        ln1_done = sem("ln1_done")
        ln_ch_done = sem("ln_ch_done")
        elu_x_done = sem("elu_x_done")
        elu_m_done = sem("elu_m_done")
        exp_done = sem("exp_done")
        elu_done = sem("elu_done")
        ksum_done = sem("ksum_done")
        kmean_done = sem("kmean_done")
        krot_done = sem("krot_done")
        kvb_done = sem("kvb_done")
        kvc_done = sem("kvc_done")
        kvs_done = sem("kvs_done")
        qrot_done = sem("qrot_done")
        den_done = sem("den_done")
        z_done = sem("z_done")
        attn_done = sem("attn_done")
        u_bias = sem("u_bias")
        lepe_step = sem("lepe_step")
        t2_done = sem("t2_done")
        ln2_step = sem("ln2_step")
        ln2_rsqrt = sem("ln2_rsqrt")
        ln2_done = sem("ln2_done")
        r_done = sem("r_done")
        csum_done = sem("csum_done")
        ll_done = sem("ll_done")
        gelu_done = sem("gelu_done")
        band_done = sem("band_done")
        r_ch_done = sem("r_ch_done")
        out_done = sem("out_done")

        LOADS = 7 * DMA
        READ = {
            "w1": (weights_ready, 0, lambda n: 2 + n),
            "gn": (gn_step, 10, lambda n: 5),
            "pq0": (lo_done, 8, lambda n: 1 + n), "pk0": (lo_done, 8, lambda n: 3 + n),
            "pq1": (lo_done, 8, lambda n: 5 + n), "pk1": (lo_done, 8, lambda n: 7 + n),
            "pv0": (v_done, 4, lambda n: 1 + n), "pv1": (v_done, 4, lambda n: 3 + n),
            "proj": (x1_done, 4, lambda n: 1 + n), "x1T": (ln1_done, 4, lambda n: 1 + n),
            "lnT": (ln_ch_done, 4, lambda n: 1 + n),
            "k": (elu_x_done, 8, lambda n: 1 + n), "q": (elu_x_done, 8, lambda n: 5 + n),
            "kT": (krot_done, 4, lambda n: 1 + n), "kv": (kvc_done, 2, lambda n: 1 + n),
            "kv2": (kvs_done, 2, lambda n: 1 + n), "den": (den_done, 1, lambda n: 1),
            "out": (attn_done, 4, lambda n: 1 + n), "uT": (t2_done, 4, lambda n: 1 + n),
            "ll": (ll_done, 1, lambda n: 1), "fc1": (gelu_done, 8, lambda n: 1 + n),
            "fc2": (band_done, 1, lambda n: 1), "rT": (r_ch_done, 4, lambda n: 1 + n),
            "up": (out_done, 2, lambda n: 1 + n),
        }

        def image_of(i, tile):
            return i + AHEAD.get(tile[0], -1)

        block = ctx.enter_context(nc.Block())

        def bodies(eng, prologue, body, epilogue):
            prologue()
            body("first", 0, False, True)
            with eng.Fori(1, B - 1) as i:
                body("steady", i, True, True)
            body("last", B - 1, True, False)
            epilogue()

        @block.sync
        def _(sp):
            def load_image(b):
                if isinstance(b, int) and b == 0:
                    pass
                else:
                    sp.wait_ge(made["pv1"], 2 * b)
                sp.dma_start(xg[:, :, :], x_v[b]).then_inc(x_in, DMA)

            def load_residual(b):
                if not (isinstance(b, int) and b == 0):
                    sp.wait_ge(stored, NC * DMA * b)
                sp.dma_start(x1[:, :, :], x_v[b]).then_inc(xres_in, DMA)

            def stack_q(b, g):
                sp.wait_ge(lo_done, 8 * b + 4 * g + 2)
                for h in range(HG):
                    for row, part in enumerate((hi, hi, lo, lo)):
                        sp.dma_start(q_st[g][D * row:D * row + D, h, :].bitcast(F32),
                                     part[D * h:D * h + D, :].bitcast(F32)).then_inc(q_stacked, DMA)

            def stack_k(b, g, half, done_units=None):
                if half == 0:
                    sp.wait_ge(lo_done, 8 * b + 4 * g + 4)
                elif done_units is not None:
                    sp.wait_ge(scores_ready, done_units)
                cols = slice(half * HALF, half * HALF + HALF)
                signal = k_stacked_b if half else k_stacked_a
                for h in range(HG):
                    for row, part in enumerate((hi, lo, hi, lo)):
                        sp.dma_start(k_st[D * row:D * row + D, h, cols].bitcast(F32),
                                     part[D * h:D * h + D, cols].bitcast(F32)).then_inc(signal, DMA)

            def store(b, c):
                sp.wait_ge(out_done, 2 * b + c + 1)
                sp.dma_start(out_v[b][:, c], x1[:, c, :]).then_inc(stored, DMA)

            def prologue():
                load_image(0)
                for dst, src in ((con[:, :], consts), (par[:, :], params), (w_qkv[:, :, :], wqkv_t),
                                 (fc1_nat, fc1_t), (w_qk[:, :, :], wqk), (w_proj[:, :, :], wproj_t),
                                 (w2[:, :, :], fc2_t)):
                    sp.dma_start(dst, src).then_inc(weights_in, DMA)
                stack_q(0, 0)
                stack_k(0, 0, 0)
                stack_k(0, 0, 1)

            def body(kind, i, post, ahead):
                if kind != "first":
                    stack_k(i, 0, 1, UNITS * i)
                stack_q(i, 1)
                stack_k(i, 1, 0)
                if ahead:
                    load_image(i + 1)
                stack_k(i, 1, 1, UNITS * i + PHASE)
                if ahead:
                    stack_q(i + 1, 0)
                    stack_k(i + 1, 0, 0)
                if post:
                    for c in range(NC):
                        store(i - 1, c)
                load_residual(i)

            def epilogue():
                for c in range(NC):
                    store(B - 1, c)
                sp.wait_ge(stored, NC * DMA * B)

            bodies(sp, prologue, body, epilogue)

        @block.tensor
        def _(pe):
            def claim(kind, i, tile):
                before, earlier = tile_before(kind, tile)
                if before is None:
                    return
                signal, per_image, after = READ[before[0]]
                pe.wait_ge(signal, per_image * image_of(i - earlier, before) + after(before[1]))

            def scores(i, s):
                g, j, h = s // PHASE, s % PHASE // HG, s % HG
                if s % PHASE == 0:
                    pe.wait_ge(q_stacked, 16 * DMA * (2 * i + g + 1))
                    pe.wait_ge(k_stacked_a, 16 * DMA * (2 * i + g + 1))
                if s % PHASE == PHASE // 2:
                    pe.wait_ge(k_stacked_b, 16 * DMA * (2 * i + g + 1))
                if s >= 2 or not (isinstance(i, int) and i == 0):
                    pe.wait_ge(probs_ready, UNITS * i + s - 1)
                for half in range(2):
                    mm = pe.matmul(ps_s[s % 2][:, half * HALF:half * HALF + HALF],
                                   k_st[:, h, j * P:j * P + P],
                                   q_st[g][:, h, half * HALF:half * HALF + HALF], start=True, stop=True)
                mm.then_inc(scores_ready, 1)

            def weigh_values(i, g, j):
                n = 2 * NB * i + NB * g + j
                pe.wait_ge(v_scaled_ready, n + 1)
                if j == 0 and not (isinstance(i, int) and i == 0 and g == 0):
                    pe.wait_ge(att_done, 4 * i + 2 * g)
                for half in range(2):
                    cols = slice(half * HALF, half * HALF + HALF)
                    for h in range(HG):
                        mm = pe.matmul(ps_o[D * h:D * h + D, cols], v_scaled[:, j % 2, D * h:D * h + D],
                                       probs[:, j % 2, h, cols], start=(j == 0), stop=(j == NB - 1))
                mm.then_inc(pv_done, 1)

            def project_heads(kind, i, tile):
                name, half = tile
                g = int(name[2])
                col = (0 if name[1] == "q" else C) + P * g
                b = image_of(i, tile)
                pe.wait_ge(gn_done, NC * (b + 1))
                for c in range(NC):
                    mm = pe.matmul(bank(tile)[:, :], w_qkv[:, c, col:col + P],
                                   xg[:, c, half * HALF:half * HALF + HALF], start=(c == 0), stop=(c == NC - 1))
                mm.then_inc(made[name], 1)

            def project_values(kind, i, tile):
                name, part = tile
                col = 2 * C + P * int(name[2])
                pe.wait_ge(gn_done, NC * (image_of(i, tile) + 1))
                for n in range(4):
                    nb = 4 * part + n
                    for c in range(NC):
                        mm = pe.matmul(bank(tile)[:, P * n:P * n + P], xg[:, c, P * nb:P * nb + P],
                                       w_qkv[:, c, col:col + P], start=(c == 0), stop=(c == NC - 1))
                mm.then_inc(made[name], 1)

            def group_means(kind, i, tile):
                pe.wait_ge(gn_step, 10 * image_of(i, tile) + 4)
                pe.matmul(bank(tile)[:, 0:2 * NC], const("gn_mean"),
                          gn_mom[:, :, :].rearrange("p c t -> p (c t)"), start=True, stop=True)\
                  .then_inc(made["gn"], 1)

            def to_tokens(tile, src, wait):
                for n in range(2):
                    for c in range(NC):
                        nb = 2 * tile[1] + n
                        mm = pe.transpose(bank(tile)[:, C * n + P * c:C * n + P * c + P],
                                          src[:, c, P * nb:P * nb + P], const("ident"))
                mm.then_inc(made[tile[0]], 1)

            def to_channels(tile, src):
                c, half = tile[1] % 2, tile[1] // 2
                for n in range(4):
                    mm = pe.transpose(bank(tile)[:, P * n:P * n + P],
                                      src[:, 4 * half + n, P * c:P * c + P], const("ident"))
                mm.then_inc(made[tile[0]], 1)

            def post_tile(kind, i, tile):
                name, n = tile
                b = image_of(i, tile)
                ps = bank(tile)
                if name == "proj":
                    c, half = n % 2, n // 2
                    pe.wait_ge(att_done, 4 * (b + 1))
                    for g in range(NG):
                        mm = pe.matmul(ps[:, :], w_proj[:, g, P * c:P * c + P],
                                       att[:, g, half * HALF:half * HALF + HALF], start=(g == 0), stop=(g == 1))
                    mm.then_inc(made[name], 1)
                elif name == "x1T":
                    pe.wait_ge(x1_done, 4 * b + 2 * (n // 2) + 2)
                    to_tokens(tile, x1, None)
                elif name == "lnT":
                    pe.wait_ge(ln1_done, 4 * b + 2 * (n // 2) + 2)
                    to_channels(tile, tok)
                elif name in ("k", "q"):
                    g, half = (n % 2, n // 2) if name == "k" else (n // 2, n % 2)
                    pe.wait_ge(ln_ch_done, 4 * b + 2 * half + 2)
                    col = (C if name == "k" else 0) + P * g
                    for c in range(NC):
                        mm = pe.matmul(ps[:, :], w_qk[:, c, col:col + P],
                                       ln_ch[:, c, 1 + half * HALF:1 + half * HALF + HALF],
                                       start=(c == 0), stop=(c == NC - 1))
                    mm.then_inc(made[name], 1)
                elif name == "kT":
                    g, half = n // 2, n % 2
                    pe.wait_ge(elu_done, 8 * b + 2 * half + g + 1)
                    for t in range(4):
                        nb = 4 * half + t
                        mm = pe.transpose(ps[:, P * t:P * t + P], qk_ch[:, g, P * nb:P * nb + P], const("ident"))
                    mm.then_inc(made[name], 1)
                elif name == "kv":
                    pe.wait_ge(krot_done, 4 * b + 2 * n + 2)
                    for r, at in ((1, P), (0, 0)):
                        for nb in range(NB):
                            mm = pe.matmul(ps[:, at:at + P], rot_tok[:, r, nb, :], tok[:, nb, P * n:P * n + P],
                                           start=(nb == 0), stop=(r == 1 and nb == NB - 1))
                    mm.then_inc(kv_half, 1)
                elif name == "kv2":
                    pe.wait_ge(kvc_done, 2 * b + n + 1)
                    pe.matmul(ps[:, 0:P], const("rot"), kv_c[:, n, :], start=True, stop=True)\
                      .then_inc(made[name], 1)
                elif name == "den":
                    pe.wait_ge(elu_done, 8 * b + 8)
                    pe.wait_ge(kmean_done, 2 * (b + 1))
                    for nb in range(NB):
                        for g in range(NG):
                            at = HG * (NG * nb + g)
                            mm = pe.matmul(ps[:, at:at + HG], qk_ch[:, g, P * nb:P * nb + P],
                                           kmean[:, g, :], start=True, stop=True)
                    mm.then_inc(made[name], 1)
                elif name == "out":
                    g, half = n // 2, n % 2
                    pe.wait_ge(qrot_done, 4 * b + n + 1)
                    pe.wait_ge(kvs_done, 2 * b + g + 1)
                    for t in range(4):
                        nb = 4 * half + t
                        for r, kv in enumerate((kv_c, kv_s)):
                            mm = pe.matmul(ps[:, P * t:P * t + P], rot_ch[:, r, P * nb:P * nb + P], kv[:, g, :],
                                           start=(r == 0), stop=(r == 1))
                    mm.then_inc(made[name], 1)
                elif name == "uT":
                    pe.wait_ge(lepe_step, 6 * (b + 1))
                    to_tokens(tile, x1, None)
                elif name == "ll":
                    pe.wait_ge(csum_done, 4 * (b + 1))
                    for nb in range(NB):
                        mm = pe.matmul(ps[:, 64 * nb:64 * nb + 64], csum[:, nb, :], const("pair_rows"),
                                       start=True, stop=True)
                    mm.then_inc(made[name], 1)
                elif name == "fc1":
                    pe.wait_ge(ll_done, b + 1)
                    pe.matmul(ps[:, :], w1[:, P * n:P * n + P], band[:, :], start=True, stop=True)\
                      .then_inc(made[name], 1)
                elif name == "fc2":
                    pe.wait_ge(gelu_done, 8 * (b + 1))
                    for k in range(HID // P):
                        mm = pe.matmul(ps[:, :], w2[:, k, :], hid[:, k, :], start=(k == 0), stop=(k == 7))
                    mm.then_inc(made[name], 1)
                elif name == "rT":
                    pe.wait_ge(r_done, 4 * b + 2 * (n // 2) + 2)
                    to_channels(tile, t2)
                elif name == "up":
                    pe.wait_ge(band_done, b + 1)
                    pe.matmul(ps[:, :], const("spread")[:, P * n:P * n + P], band[:, :], start=True, stop=True)\
                      .then_inc(made[name], 1)

            def kv_rotate(i, n):
                b = i - 1
                pe.wait_ge(kvb_done, 2 * b + n + 1)
                pe.matmul(bank(("kv", n))[:, 0:P], const("rot_t"), kv_b[:, n, :], start=False, stop=True)\
                  .then_inc(made["kv"], 1)

            def post_slot(kind, i, s):
                if s in (23, 27):
                    kv_rotate(i, (s - 23) // 4)
                for tile in POST_AT.get(s, []):
                    claim(kind, i, tile)
                    post_tile(kind, i, tile)

            def pre_tile(kind, i, tile):
                claim(kind, i, tile)
                {"g": group_means, "q": project_heads, "k": project_heads,
                 "v": project_values}[tile[0][0 if tile[0] == "gn" else 1]](kind, i, tile)

            def prologue():
                pe.wait_ge(weights_in, LOADS)
                for half in range(2):
                    for c in range(NC):
                        mm = pe.matmul(work[half][:, :], const("interp")[:, LL * c:LL * c + LL],
                                       fc1_nat[:, c, half * HALF:half * HALF + HALF],
                                       start=(c == 0), stop=(c == NC - 1))
                    mm.then_inc(made["w1"], 1)
                pe.wait_ge(weights_ready, 1)
                for tiles in PRE0_AT.values():
                    for tile in tiles:
                        pre_tile("prologue", -1, tile)
                scores(0, 0)

            def body(kind, i, post, ahead):
                for s in range(UNITS):
                    if s + 1 < UNITS:
                        scores(i, s + 1)
                    elif ahead:
                        scores(i + 1, 0)
                    if post:
                        post_slot(kind, i, s)
                    for tile in PRE1_AT.get(s, []):
                        pre_tile(kind, i, tile)
                    for tile in PRE0_AT.get(s, []) if ahead else []:
                        pre_tile(kind, i, tile)
                    if s % HG == 2:
                        n = s // HG - 1
                        if n >= 0:
                            weigh_values(i, n // NB, n % NB)
                        elif kind != "first":
                            weigh_values(i - 1, NG - 1, NB - 1)

            def epilogue():
                weigh_values(B - 1, NG - 1, NB - 1)
                for s in range(UNITS):
                    post_slot("epilogue", B, s)

            bodies(pe, prologue, body, epilogue)

        @block.scalar
        def _(act):
            def exponentials(i, s):
                j, h = s % PHASE // HG, s % HG
                if s >= 2 * HG or not (isinstance(i, int) and i == 0):
                    act.wait_ge(pv_done, 2 * NB * i + s // HG - 1)
                act.wait_ge(max_ready, UNITS * i + s + 1)
                act.activation(probs[:, j % 2, h, :], ps_s[s % 2][:, :], ACT.Exp, bias=negmax[:, s % 4:s % 4 + 1],
                               accum_out=sums[:, j % 2, h:h + 1]).then_inc(probs_ready, 1)

            def copy_attention(i, g):
                act.wait_ge(pv_done, 2 * NB * i + NB * (g + 1))
                if not (isinstance(i, int) and i == 0):
                    act.wait_ge(made["proj"], 4 * i)
                for half in range(2):
                    cols = slice(half * HALF, half * HALF + HALF)
                    act.copy(att[:, g, cols], ps_o[:, cols]).then_inc(att_done, 1)

            def gn_apply(b, c):
                act.wait_ge(gn_step, 10 * b + 10)
                act.activation(xg[:, c, :], xg[:, c, :], ACT.Identity, bias=gn_sh[:, c:c + 1],
                               scale=gn_a[:, c:c + 1]).then_inc(gn_done, 1)

            def lepe_bias(b, c):
                act.wait_ge(made["x1T"], 4 * (b + 1))
                act.activation(x1[:, c, :], x1[:, c, :], ACT.Identity, bias=param("lepe_b", c)).then_inc(u_bias, 1)

            def high_part(i, tile):
                name, half = tile
                g, b = int(name[2]), image_of(i, tile)
                is_k = name[1] == "k"
                done = 2 * b + g
                if not (isinstance(done, int) and done == 0) or is_k:
                    if is_k:
                        act.wait_ge(q_stacked, 16 * DMA * (done + 1))
                    else:
                        act.wait_ge(k_stacked_b, 16 * DMA * done)
                act.wait_ge(made[name], 2 * b + half + 1)
                act.activation(hi[:, half * HALF:half * HALF + HALF], bank(tile)[:, :], ACT.Identity,
                               bias=param("bk" if is_k else "bq", g)).then_inc(hi_done, 1)

            def post_tile(i, tile):
                name, n = tile
                b = image_of(i, tile)
                ps = bank(tile)
                if name == "lnT":
                    c, half = n % 2, n // 2
                    act.wait_ge(made[name], 4 * b + n + 1)
                    act.copy(ln_ch[:, c, 1 + half * HALF:1 + half * HALF + HALF], ps[:, :])\
                       .then_inc(ln_ch_done, 1)
                elif name in ("k", "q"):
                    g = n % 2 if name == "k" else n // 2
                    col = (NG if name == "k" else 0) + g
                    m = (0 if name == "k" else 4) + n
                    if m >= 2:
                        act.wait_ge(elu_done, 8 * b + m - 1)
                    act.wait_ge(made[name], 4 * b + n + 1)
                    act.activation(elu_x[:, n % 2, :], ps[:, :], ACT.Identity, bias=param("bqk", col))\
                       .then_inc(elu_x_done, 1)
                elif name == "ll":
                    act.wait_ge(made[name], b + 1)
                    act.copy(band[:, :], ps[:, :]).then_inc(ll_done, 1)
                elif name == "fc1":
                    act.wait_ge(made[name], 8 * b + n + 1)
                    act.activation(hid[:, n, :], ps[:, :], ACT.Gelu, bias=param("b1", n)).then_inc(gelu_done, 1)
                elif name == "rT":
                    c, half = n % 2, n // 2
                    act.wait_ge(made[name], 4 * b + n + 1)
                    act.copy(x1[:, c, half * HALF:half * HALF + HALF], ps[:, :]).then_inc(r_ch_done, 1)

            def elu_exp(b, m):
                act.wait_ge(elu_m_done, 8 * b + m + 1)
                act.activation(elu_e[:, m % 2, :], elu_e[:, m % 2, :], ACT.Exp).then_inc(exp_done, 1)

            def post_slot(i, s):
                if s in ELU_AT:
                    elu_exp(i - 1, ELU_AT[s])
                for tile in POST_AT.get(s, []):
                    post_tile(i, tile)
                if s in (20, 21):
                    lepe_bias(i - 1, s - 20)
                if s in (22, 26):
                    n = (s - 22) // 4
                    act.wait_ge(kv_half, 2 * (i - 1) + n + 1)
                    act.copy(kv_b[:, n, :], bank(("kv", n))[:, P:2 * P]).then_inc(kvb_done, 1)

            def pre_slot(i, at, s):
                for tile in at.get(s, []):
                    if tile[0][1] in "qk":
                        high_part(i, tile)

            def prologue():
                act.wait_ge(weights_ready, 1)
                for s in range(UNITS):
                    if s in (40, 41):
                        gn_apply(0, s - 40)
                    pre_slot(-1, PRE0_AT, s)

            def body(kind, i, post, ahead):
                for s in range(UNITS):
                    exponentials(i, s)
                    if s == 3 and kind != "first":
                        copy_attention(i - 1, 1)
                    if s == PHASE + 3:
                        copy_attention(i, 0)
                    if post:
                        post_slot(i, s)
                    pre_slot(i, PRE1_AT, s)
                    if ahead:
                        if s in (40, 41):
                            gn_apply(i + 1, s - 40)
                        pre_slot(i, PRE0_AT, s)

            def epilogue():
                copy_attention(B - 1, 1)
                for s in range(UNITS):
                    post_slot(B, s)

            bodies(act, prologue, body, epilogue)

        @block.vector
        def _(dve):
            def carry_wait():
                dve.memset(wait_carrier[:, :], 0.0)

            def maximum(i, s):
                dve.wait_ge(scores_ready, UNITS * i + s + 1)
                dve.tensor_reduce(negmax[:, s % 4:s % 4 + 1], ps_s[s % 2][:, :], AX_X, ALU.max, negate=True)\
                   .then_inc(max_ready, 1)

            def invert_sums(i, g, j):
                n = NB * g + j
                dve.wait_ge(probs_ready, UNITS * i + HG * (n + 1))
                dve.reciprocal(rsums[:, j % 2, :], sums[:, j % 2, :]).then_inc(rsums_ready, 1)

            def gn_statistics(b, c):
                dve.wait_ge(x_in, DMA * (b + 1))
                for half in range(2):
                    st = dve.bn_stats(gn_stats[:, c, half, :], xg[:, c, half * HALF:half * HALF + HALF])
                if c == NC - 1:
                    st.then_inc(gn_step, 1)

            def gn_moments(b):
                dve.wait_ge(gn_step, 10 * b + 1)
                carry_wait()
                for c in range(NC):
                    ag = dve.bn_aggr(gn_mom[:, c, :], gn_stats[:, c, :, :].rearrange("p a s -> p (a s)"))
                ag.then_inc(gn_step, 1)
                dve.wait_ge(gn_step, 10 * b + 2)
                dve.tensor_tensor(gn_sq[:, :], gn_mom[:, :, 0], gn_mom[:, :, 0], ALU.mult).then_inc(gn_step, 1)
                dve.wait_ge(gn_step, 10 * b + 3)
                dve.tensor_tensor(gn_mom[:, :, 1], gn_mom[:, :, 1], gn_sq[:, :], ALU.add).then_inc(gn_step, 1)

            def gn_variance(b):
                dve.wait_ge(made["gn"], b + 1)
                dve.tensor_copy(gn_grp[:, :, :].rearrange("p c t -> p (c t)"), bank(("gn", 0))[:, 0:2 * NC])\
                   .then_inc(gn_step, 1)
                dve.wait_ge(gn_step, 10 * b + 5)
                dve.tensor_tensor(gn_sq[:, :], gn_grp[:, :, 0], gn_grp[:, :, 0], ALU.mult).then_inc(gn_step, 1)
                dve.wait_ge(gn_step, 10 * b + 6)
                dve.scalar_tensor_tensor(out=gn_var[:, :], in0=gn_grp[:, :, 1], scalar=1e-5, in1=gn_sq[:, :],
                                         op0=ALU.add, op1=ALU.subtract).then_inc(gn_step, 1)

            def gn_affine(b):
                dve.wait_ge(gn_rsqrt, b + 1)
                dve.tensor_tensor(gn_a[:, :], gn_rs[:, :], param("gn_w"), ALU.mult).then_inc(gn_step, 1)
                dve.wait_ge(gn_step, 10 * b + 8)
                dve.tensor_tensor(gn_ma[:, :], gn_grp[:, :, 0], gn_a[:, :], ALU.mult).then_inc(gn_step, 1)
                dve.wait_ge(gn_step, 10 * b + 9)
                dve.tensor_tensor(gn_sh[:, :], param("gn_b"), gn_ma[:, :], ALU.subtract).then_inc(gn_step, 1)

            def low_part(i, tile):
                name, half = tile
                g, b = int(name[2]), image_of(i, tile)
                is_k = name[1] == "k"
                dve.wait_ge(hi_done, 8 * b + 4 * g + (2 if is_k else 0) + half + 1)
                cols = slice(half * HALF, half * HALF + HALF)
                dve.scalar_tensor_tensor(out=lo[:, cols], in0=bank(tile)[:, :],
                                         scalar=param("bk" if is_k else "bq", g),
                                         in1=hi[:, cols].bitcast(F32), op0=ALU.add, op1=ALU.subtract)\
                   .then_inc(lo_done, 1)

            def values(i, tile):
                name, part = tile
                g, b = int(name[2]), image_of(i, tile)
                if not (isinstance(b, int) and b == 0):
                    dve.wait_ge(v_scaled_ready, 2 * NB * (b - 1) + NB * (g + 1))
                dve.wait_ge(made[name], 2 * b + part + 1)
                bias = param("bv")[:, P * g:P * g + P].rearrange("p (o c) -> p o c", o=1)
                dve.tensor_tensor(v_tok[g][:, 4 * part:4 * part + 4, :],
                                  bank(tile)[:, :].rearrange("p (n c) -> p n c", n=4),
                                  bias.to_broadcast([P, 4, P]), ALU.add).then_inc(v_done, 1)

            def ln_statistics(b, n, src, step):
                for t in range(2):
                    st = dve.bn_stats(ln_st[:, t, :], src(t))
                st.then_inc(step, 1)
                dve.wait_ge(step, 12 * b + 3 * n + 1)
                carry_wait()
                for t in range(2):
                    ag = dve.bn_aggr(ln_mv[:, n, t, :], ln_st[:, t, :])
                ag.then_inc(step, 1)
                dve.wait_ge(step, 12 * b + 3 * n + 2)
                dve.tensor_scalar(ln_var[:, n, :], ln_mv[:, n, :, 1], 1e-5, None, ALU.add).then_inc(step, 1)

            def ln_normalise(b, n, src, rsqrt, done):
                dve.wait_ge(rsqrt, 4 * b + n + 1)
                for t in range(2):
                    nm = dve.tensor_scalar(tok[:, 2 * n + t, :], src(t), ln_mv[:, n, t, 0:1],
                                           ln_rs[:, n, t:t + 1], ALU.subtract, ALU.mult)
                nm.then_inc(done, 1)

            def x1_tokens(n):
                return lambda t: bank(("x1T", n))[:, C * t:C * t + C]

            def t2_tokens(n):
                return lambda t: t2[:, 2 * n + t, :]

            def four_heads(ap):
                return ap.rearrange("p (n h d) -> p n h d", n=4, h=HG)

            def post_tile(i, tile):
                name, n = tile
                b = image_of(i, tile)
                ps = bank(tile)
                if name == "proj":
                    c, half = n % 2, n // 2
                    cols = slice(half * HALF, half * HALF + HALF)
                    dve.wait_ge(xres_in, DMA * (b + 1))
                    dve.wait_ge(made[name], 4 * b + n + 1)
                    dve.scalar_tensor_tensor(out=x1[:, c, cols], in0=ps[:, :], scalar=param("bproj", c),
                                             in1=x1[:, c, cols], op0=ALU.add, op1=ALU.add).then_inc(x1_done, 1)
                elif name == "x1T":
                    dve.wait_ge(made[name], 4 * b + n + 1)
                    ln_statistics(b, n, x1_tokens(n), ln1_step)
                elif name in ("k", "q"):
                    dve.wait_ge(elu_x_done, 8 * b + (4 if name == "q" else 0) + n + 1)
                    dve.tensor_scalar(elu_e[:, n % 2, :], elu_x[:, n % 2, :], 0.0, None, ALU.min)\
                       .then_inc(elu_m_done, 1)
                elif name == "kT":
                    g, half = n // 2, n % 2
                    if g == 1:
                        dve.wait_ge(kv_half, 2 * b + 1)
                    dve.wait_ge(made[name], 4 * b + n + 1)
                    for r, table in enumerate(("cos_tok", "sin_tok")):
                        tab = const(table)[:, 4 * D * half:4 * D * half + 4 * D]\
                            .rearrange("p (n o d) -> p n o d", n=4, o=1).to_broadcast([P, 4, HG, D])
                        dst = rot_tok[:, r, 4 * half:4 * half + 4, :].rearrange("p n (h d) -> p n h d", h=HG)
                        mu = dve.tensor_tensor(dst, four_heads(ps[:, :]), tab, ALU.mult)
                    mu.then_inc(krot_done, 1)
                elif name == "kv2":
                    dve.wait_ge(made[name], 2 * b + n + 1)
                    dve.tensor_copy(kv_s[:, n, :], ps[:, 0:P]).then_inc(kvs_done, 1)
                elif name == "den":
                    dve.wait_ge(made[name], b + 1)
                    dve.tensor_scalar(den[:, :], ps[:, 0:NB * NG * HG], 1e-6, None, ALU.add).then_inc(den_done, 1)
                    dve.wait_ge(den_done, b + 1)
                    dve.reciprocal(zden[:, :, :, :].rearrange("p n g h -> p (n g h)"), den[:, :])\
                       .then_inc(z_done, 1)
                elif name == "out":
                    g, half = n // 2, n % 2
                    dve.wait_ge(z_done, b + 1)
                    dve.wait_ge(made[name], 4 * b + n + 1)
                    z = zden[:, 4 * half:4 * half + 4, g, :].rearrange("p n (h o) -> p n h o", o=1)
                    dst = t2[:, 4 * half:4 * half + 4, P * g:P * g + P].rearrange("p n (h d) -> p n h d", h=HG)
                    dve.tensor_tensor(dst, four_heads(ps[:, :]), z.to_broadcast([P, 4, HG, D]), ALU.mult)\
                       .then_inc(attn_done, 1)
                elif name == "uT":
                    dve.wait_ge(attn_done, 4 * (b + 1))
                    dve.wait_ge(made[name], 4 * b + n + 1)
                    both = t2[:, 2 * n:2 * n + 2, :]
                    dve.tensor_tensor(both, ps[:, :].rearrange("p (n c) -> p n c", n=2), both, ALU.add)\
                       .then_inc(t2_done, 1)
                    dve.wait_ge(t2_done, 4 * b + n + 1)
                    ln_statistics(b, n, t2_tokens(n), ln2_step)
                elif name == "fc2":
                    dve.wait_ge(made[name], b + 1)
                    dve.scalar_tensor_tensor(out=band[:, :], in0=ps[:, :], scalar=param("b2"), in1=band[:, :],
                                             op0=ALU.add, op1=ALU.subtract).then_inc(band_done, 1)
                elif name == "up":
                    dve.wait_ge(r_ch_done, 4 * (b + 1))
                    dve.wait_ge(made[name], 2 * b + n + 1)
                    pairs = x1[:, n, :].rearrange("p (m t) -> p m t", t=2)
                    up = ps[:, :].rearrange("p (m o) -> p m o", o=1).to_broadcast([P, HALF, 2])
                    dve.tensor_tensor(pairs, up, pairs, ALU.add).then_inc(out_done, 1)

            def elu(b, m):
                is_q, n = m // 4, m % 4
                g, half = (n // 2, n % 2) if is_q else (n % 2, n // 2)
                if m == 4:
                    dve.wait_ge(made["kT"], 4 * (b + 1))
                dve.wait_ge(exp_done, 8 * b + m + 1)
                dve.scalar_tensor_tensor(out=qk_ch[:, g, half * HALF:half * HALF + HALF],
                                         in0=elu_x[:, m % 2, :], scalar=1.0, in1=elu_e[:, m % 2, :],
                                         op0=ALU.add, op1=ALU.max,
                                         accum_out=None if is_q else ksum[:, n:n + 1]).then_inc(elu_done, 1)

            def lepe(b, c, tap):
                if c == 0 and tap == 0:
                    dve.wait_ge(edges_zero, 2)
                    dve.wait_ge(ln_ch_done, 4 * (b + 1))
                dve.wait_ge(u_bias, 2 * b + c + 1)
                if tap > 0:
                    dve.wait_ge(lepe_step, 6 * b + 3 * c + tap)
                dve.scalar_tensor_tensor(out=x1[:, c, :], in0=ln_ch[:, c, tap:tap + L],
                                         scalar=param("lepe_w", 3 * c + tap), in1=x1[:, c, :],
                                         op0=ALU.mult, op1=ALU.add).then_inc(lepe_step, 1)

            LEPE_AT = {28: (0, 0), 30: (0, 1), 32: (0, 2), 35: (1, 0), 36: (1, 1), 37: (1, 2)}

            def post_slot(i, s):
                b = i - 1
                if s in (9, 10, 11, 12):
                    ln_normalise(b, s - 9, x1_tokens(s - 9), ln1_rsqrt, ln1_done)
                if s in (41, 42, 43, 44):
                    ln_normalise(b, s - 41, t2_tokens(s - 41), ln2_rsqrt, ln2_done)
                if s in ELU_AT:
                    elu(b, ELU_AT[s])
                if s in (23, 27):
                    n = (s - 23) // 4
                    dve.wait_ge(made["kv"], 2 * b + n + 1)
                    dve.tensor_tensor(kv_c[:, n, :], bank(("kv", n))[:, 0:P], const("head_mask"), ALU.mult)\
                       .then_inc(kvc_done, 1)
                for tile in POST_AT.get(s, []):
                    post_tile(i, tile)
                if s == 20:
                    dve.wait_ge(elu_done, 8 * b + 4)
                    dve.tensor_tensor(ksum_g[:, :], ksum[:, 0:NG], ksum[:, NG:2 * NG], ALU.add).then_inc(ksum_done, 1)
                    dve.wait_ge(ksum_done, b + 1)
                    for g in range(NG):
                        dve.tensor_scalar(kmean[:, g, :], const("head_mean"), ksum_g[:, g:g + 1], None, ALU.mult)\
                           .then_inc(kmean_done, 1)
                if s in LEPE_AT:
                    lepe(b, *LEPE_AT[s])

            def pre_slot(i, at, s):
                for tile in at.get(s, []):
                    if tile[0] == "gn":
                        gn_variance(image_of(i, tile))
                    elif tile[0][1] in "qk":
                        low_part(i, tile)
                    else:
                        values(i, tile)

            def prologue():
                dve.wait_ge(weights_in, LOADS)
                for c in range(NC):
                    dve.tensor_scalar(w_qkv[:, c, 0:C], w_qkv[:, c, 0:C], float(D) ** -0.5, None, ALU.mult)
                dve.tensor_scalar(param("bq"), param("bq"), float(D) ** -0.5, None, ALU.mult).then_inc(weights_ready, 1)
                for half in range(2):
                    dve.wait_ge(made["w1"], half + 1)
                    dve.tensor_copy(w1[:, half * HALF:half * HALF + HALF], work[half][:, :])\
                       .then_inc(weights_ready, 1)
                gn_statistics(0, 0)
                gn_statistics(0, 1)
                gn_moments(0)
                for s in range(UNITS):
                    pre_slot(-1, PRE0_AT, s)
                    if s == 39:
                        gn_affine(0)

            def body(kind, i, post, ahead):
                for s in range(UNITS):
                    maximum(i, s)
                    if s % HG == 0:
                        n = s // HG - 1
                        if n >= 0:
                            invert_sums(i, n // NB, n % NB)
                        elif kind != "first":
                            invert_sums(i - 1, NG - 1, NB - 1)
                    if post:
                        post_slot(i, s)
                    pre_slot(i, PRE1_AT, s)
                    if ahead:
                        if s in (33, 34):
                            gn_statistics(i + 1, s - 33)
                        if s == 35:
                            gn_moments(i + 1)
                        pre_slot(i, PRE0_AT, s)
                        if s == 39:
                            gn_affine(i + 1)

            def epilogue():
                invert_sums(B - 1, NG - 1, NB - 1)
                for s in range(UNITS):
                    post_slot(B, s)

            bodies(dve, prologue, body, epilogue)

        @block.gpsimd
        def _(pool):
            def scale_values(i, g, j):
                n = 2 * NB * i + NB * g + j
                pool.wait_ge(v_done, 4 * i + 2 * g + 2)
                if j >= 2 or not (isinstance(i, int) and i == 0 and g == 0):
                    pool.wait_ge(pv_done, n - 1)
                pool.wait_ge(rsums_ready, n + 1)
                r = rsums[:, j % 2, :].rearrange("p (h o) -> p h o", o=1)
                pool.tensor_tensor(v_scaled[:, j % 2, :].rearrange("p (h d) -> p h d", h=HG),
                                   v_tok[g][:, j, :].rearrange("p (h d) -> p h d", h=HG),
                                   r.to_broadcast([P, HG, D]), ALU.mult).then_inc(v_scaled_ready, 1)

            def gn_rsqrt_of(b):
                pool.wait_ge(gn_step, 10 * b + 7)
                pool.tensor_tensor(gn_rs[:, :], gn_var[:, :], const("minus_half")[:, 0:NC], ALU.pow)\
                    .then_inc(gn_rsqrt, 1)

            def rsqrt(step, b, n, done):
                pool.wait_ge(step, 12 * b + 3 * n + 3)
                pool.tensor_tensor(ln_rs[:, n, :], ln_var[:, n, :], const("minus_half")[:, 0:2], ALU.pow)\
                    .then_inc(done, 1)

            def rotate_q(b, n):
                g, half = n // 2, n % 2
                cols = slice(half * HALF, half * HALF + HALF)
                if n == 0:
                    pool.wait_ge(kv_half, 2 * (b + 1))
                if n == 2:
                    pool.wait_ge(made["out"], 4 * b + 2)
                pool.wait_ge(elu_done, 8 * b + 4 + n + 1)
                for r, table in enumerate(("cos_ch", "sin_ch")):
                    mu = pool.tensor_tensor(rot_ch[:, r, cols], qk_ch[:, g, cols], const(table)[:, cols], ALU.mult)
                mu.then_inc(qrot_done, 1)

            def after_norm(b, n):
                rows = slice(2 * n, 2 * n + 2)
                pool.wait_ge(ln2_done, 4 * b + n + 1)
                pool.tensor_tensor(t2[:, rows, :], t2[:, rows, :], tok[:, rows, :], ALU.add).then_inc(r_done, 1)
                pool.tensor_tensor(csum[:, rows, :], tok[:, rows, 0:C:2], tok[:, rows, 1:C:2], ALU.add)\
                    .then_inc(csum_done, 1)

            ROTATE_AT = {28: 0, 29: 1, 35: 2, 36: 3}

            def post_slot(i, s):
                b = i - 1
                if s in (8, 9, 10, 11):
                    rsqrt(ln1_step, b, s - 8, ln1_rsqrt)
                if s in ROTATE_AT:
                    rotate_q(b, ROTATE_AT[s])
                if s in (40, 41, 42, 43):
                    rsqrt(ln2_step, b, s - 40, ln2_rsqrt)
                if s in (41, 42, 43, 44):
                    after_norm(b, s - 41)

            def prologue():
                for col in (0, L + 1):
                    pool.memset(ln_ch[:, :, col:col + 1], 0.0).then_inc(edges_zero, 1)
                pool.wait_ge(weights_in, LOADS)
                gn_rsqrt_of(0)

            def body(kind, i, post, ahead):
                for s in range(UNITS):
                    if s % HG == 1:
                        n = s // HG - 1
                        if n >= 0:
                            scale_values(i, n // NB, n % NB)
                        elif kind != "first":
                            scale_values(i - 1, NG - 1, NB - 1)
                    if post:
                        post_slot(i, s)
                    if ahead:
                        if s == 38:
                            gn_rsqrt_of(i + 1)

            def epilogue():
                scale_values(B - 1, NG - 1, NB - 1)
                for s in range(UNITS):
                    post_slot(B, s)

            bodies(pool, prologue, body, epilogue)


def constants():
    p = np.arange(P)
    con = {n: np.zeros((P, b - a), np.float32) for n, (a, b) in CONSTS.items()}
    con["ident"][p, p] = 1
    con["gn_mean"][:] = (p[:, None] // GN_SIZE == p[None, :] // GN_SIZE) / GN_SIZE
    rot = np.zeros((P, P), np.float32)
    low = p % D < D // 2
    rot[p[low], p[low] + D // 2] = -1
    rot[p[~low], p[~low] - D // 2] = 1
    con["rot"][:] = rot
    con["rot_t"][:] = rot.T
    con["head_mask"][:] = (p[:, None] // D == p[None, :] // D) / L
    con["head_mean"][:] = (p[:, None] // D == np.arange(HG)[None, :]) / L
    con["pair_rows"][:] = 0.5 * (p[:, None] // 2 == np.arange(P // 2)[None, :])
    con["spread"][:] = 0.5 * (p[:, None] == np.arange(C)[None, :] // 2)
    pos = np.linspace(0.0, 1.0, C, dtype=np.float32) * np.float32(LL - 1)
    i0 = np.clip(np.floor(pos).astype(np.int32), 0, LL - 2)
    w = pos - i0.astype(np.float32)
    interp = np.zeros((C, LL), np.float32)
    interp[np.arange(C), i0] = np.float32(1.0) - w
    interp[np.arange(C), i0 + 1] = w
    con["interp"][:] = interp.reshape(NC, P, LL).transpose(1, 0, 2).reshape(P, NC * LL)
    con["minus_half"][:] = -0.5
    inv_freq = (1.0 / np.float32(10000.0) ** (np.arange(0, D, 2, dtype=np.float32) / np.float32(D))).astype(np.float32)
    freqs = np.outer(np.arange(L, dtype=np.float32), inv_freq).astype(np.float32)
    emb = np.concatenate([freqs, freqs], axis=-1)
    for name, table in (("cos", np.cos(emb)), ("sin", np.sin(emb))):
        con[name + "_tok"][:] = table.reshape(NB, P, D).transpose(1, 0, 2).reshape(P, NB * D)
        con[name + "_ch"][:] = np.tile(table.T, (HG, 1))
    return np.ascontiguousarray(np.concatenate([con[n] for n in CONSTS], axis=1))


def kernel(x, L0_conv_gn_w, L0_conv_gn_b, L0_conv_w_qkv, L0_conv_b_qkv, L0_conv_w_proj, L0_conv_b_proj,
           L1_attn_Wqk, L1_attn_bqk, L1_attn_lepe_w, L1_attn_lepe_b, L1_ffn_fc1_w, L1_ffn_fc1_b,
           L1_ffn_fc2_w, L1_ffn_fc2_b):
    import concourse.bacc as bacc
    from concourse.bass_utils import run_bass_kernel_spmd

    def halves(a):
        a = np.asarray(a)
        return np.ascontiguousarray(a.reshape(-1, P, a.shape[-1]).transpose(1, 0, 2))

    def columns(a):
        return np.asarray(a).reshape(-1, P).T

    heads = C // D
    w_qkv = np.asarray(L0_conv_w_qkv).reshape(heads, 3, D, C).transpose(1, 0, 2, 3).reshape(3 * C, C)
    b_qkv = np.asarray(L0_conv_b_qkv).reshape(heads, 3, D).transpose(1, 0, 2).reshape(3, C)
    lepe_w = np.asarray(L1_attn_lepe_w).reshape(NC, P, 3).transpose(1, 0, 2).reshape(P, NC * 3)
    par = {"bq": columns(b_qkv[0]), "bk": columns(b_qkv[1]), "bproj": columns(L0_conv_b_proj),
           "bqk": columns(L1_attn_bqk), "lepe_w": lepe_w, "lepe_b": columns(L1_attn_lepe_b),
           "b1": columns(L1_ffn_fc1_b), "b2": columns(L1_ffn_fc2_b), "gn_w": columns(L0_conv_gn_w),
           "gn_b": columns(L0_conv_gn_b), "bv": np.broadcast_to(b_qkv[2][None, :], (P, C))}
    arrays = {
        "x": np.ascontiguousarray(x),
        "wqkv_t": halves(w_qkv.T), "wproj_t": halves(np.asarray(L0_conv_w_proj).T), "wqk": halves(L1_attn_Wqk),
        "fc1_t": halves(np.asarray(L1_ffn_fc1_w).T), "fc2_t": halves(np.asarray(L1_ffn_fc2_w).T),
        "params": np.ascontiguousarray(np.concatenate([par[n] for n in PARAMS], axis=1)),
        "consts": constants(),
    }
    nc = bacc.Bacc("TRN2", target_bir_lowering=False, num_devices=1)
    args = [nc.dram_tensor("in_" + n, a.shape, mybir.dt.from_np(a.dtype), kind="ExternalInput").ap()
            for n, a in arrays.items()]
    args.append(nc.dram_tensor("out_x", (B, C, 32, 32), F32, kind="ExternalOutput").ap())
    build(nc, *args)
    r = run_bass_kernel_spmd(nc, [{"in_" + n: a for n, a in arrays.items()}], core_ids=[0])
    return r.results[0]["out_x"]
```

```python
from contextlib import ExitStack

import numpy as np

import concourse.bass as bass
from concourse import mybir

F32 = mybir.dt.float32
F32R = mybir.dt.float32r
ALU = mybir.AluOpType
ACT = mybir.ActivationFunctionType
AX_X = mybir.AxisListType.X

P = 128
B, C, L = 8, 256, 1024
NC = C // P
NG = 2
HG, D = 4, 32
NB = L // P
HALF = 512
HID = 1024
LL = C // 2
GN_SIZE = 8
UNITS = NG * NB * HG
PHASE = NB * HG
DMA = 16

CONSTS = {}
_at = 0
for _name, _width in (("gn_mean", P), ("minus_half", 4), ("eps", 2), ("ident", P), ("rot_t", P), ("rot", P), ("head_mask", P),
                      ("head_mean", HG), ("pair_rows", P // 2), ("spread", C), ("interp", NC * LL),
                      ("cos_tok", NB * D), ("sin_tok", NB * D),
                      ("cos_ch", L), ("sin_ch", L)):
    CONSTS[_name] = (_at, _at + _width)
    _at += _width
CONST_W = _at
EARLY = CONSTS["ident"][0]

PARAMS = {}
_at = 0
for _name, _width in (("bq", 2), ("bk", 2), ("bproj", 2), ("bqk", 4), ("lepe_w", 6), ("lepe_b", 2),
                      ("b1", 8), ("b2", 1), ("gn_w", 2), ("gn_b", 2), ("bv", C)):
    PARAMS[_name] = (_at, _at + _width)
    _at += _width
PARAM_W = _at

POST_AT = {
    4: [("proj", 0), ("proj", 1)], 7: [("x1T", 0)], 8: [("x1T", 1)], 10: [("proj", 2)],
    12: [("proj", 3), ("lnT", 0)], 13: [("x1T", 2)], 14: [("lnT", 1), ("x1T", 3)], 16: [("k", 0)],
    17: [("k", 1)], 19: [("lnT", 2), ("kT", 0)], 20: [("lnT", 3)], 24: [("k", 2)],
    25: [("k", 3), ("kT", 1)], 27: [("q", 0)], 28: [("kv", 0)], 29: [("kv close", 0)],
    30: [("kT", 2)], 31: [("kT", 3), ("q", 1)], 32: [("kv", 1)], 33: [("q", 2)],
    34: [("kv close", 1), ("kv2", 0)], 36: [("den", 0), ("kv2", 1), ("q", 3)], 37: [("out", 0)],
    39: [("out", 1), ("uT", 0)], 40: [("den", 1)], 41: [("uT", 1), ("out", 2)],
    44: [("out", 3), ("uT", 2), ("uT", 3), ("rT", 0), ("rT", 1)], 48: [("ll", 0), ("rT", 2)],
    51: [("fc1", n) for n in range(0, 8)], 52: [("rT", 3), ("fc2", 0)], 53: [("fc2", 1)],
    54: [("fc2", 2)], 58: [("fc2", 3)], 60: [("up", 0), ("up", 1)],
}
PRE1_AT = {
    0: [("pv1", 0)], 2: [("pv1", 1)], 6: [("pq1", 0)], 9: [("pq1", 1)],
    21: [("pk1", 0), ("pk1", 1)],
}
PRE0_AT = {
    35: [("gn", 0)], 45: [("pq0", 0)], 46: [("pq0", 1)], 53: [("pk0", 0)], 56: [("pk0", 1)],
    61: [("pv0", 0), ("pv0", 1)],
}
CLOSES = {("kv", 0): ("kv close", 0), ("kv", 1): ("kv close", 1), ("fc2", 0): ("fc2", 3)}
LATER_STEPS = [("kv close", 0), ("kv close", 1), ("fc2", 1), ("fc2", 2), ("fc2", 3)]
ACT_LAG = {
    "x1T": 0, "lnT": 0, "k": 0, "q": 1, "kv": 0, "rT": 1, "ll": 1, "fc1": 0, "pk1": 0, "pq1": 0,
    "pq0": 1, "pk0": 1, ("x1T", 0): 1, ("q", 0): 0, ("kv", 1): 1, ("pq1", 1): 1,
}
DVE_LAG = {
    "proj": 1, "x1T": 3, "k": 2, "kT": 1, "q": 2, "kv close": 1, "kv2": 1, "den": 1, "out": 1,
    "uT": 1, "fc2": 1, "up": 1, "pv1": 3, "pk1": 2, "pq1": 2, "pv0": 0, "pq0": 2, "gn": 1,
    "pk0": 2, ("x1T", 1): 2, ("x1T", 2): 2, ("k", 0): 3, ("kT", 1): 2, ("kT", 3): 0,
    ("kv close", 1): 0, ("out", 2): 2, ("fc2", 0): 0, ("fc2", 2): 2, ("pv1", 1): 2, ("pv0", 1): 1,
}
DVE_NORM_LAG = {
    "x1T": 4, "uT": 2, ("x1T", 0): 5, ("uT", 1): 4, ("uT", 3): 3,
}
POOL_LAG = {
    "x1T": 4, "uT": 2, "gn": 0, ("x1T", 2): 3, ("x1T", 3): 2, ("uT", 0): 0, ("uT", 3): 3,
}
POOL_SUM_LAG = {
    "uT": 3, ("uT", 2): 4, ("uT", 3): 4,
}
LEPE_BIAS_AT = {15: 0, 18: 1}
LEPE_DVE_AT = {21: 0, 25: 1, 32: 2}
LEPE_POOL_AT = {21: 0, 22: 1, 23: 2, 25: 3, 29: 4, 36: 5}
ROTATE_AT = {33: 0, 36: 1, 38: 2, 42: 3}
KMEAN_AT = 27
LOAD_AT = 26
GN_STATS_AT = {30: [0], 31: [1], 32: [2], 35: [3]}
GN_MOMENTS_AT = 35
GN_APPLY_AT = {39: 0, 42: 1}
FOLD_AT = {
    20: [("w1", 0)], 22: [("w1", 1)],
}


def lagged(table, lag):
    out = {}
    for s in sorted(table):
        for tile in table[s]:
            n = lag.get(tile, lag.get(tile[0]))
            if n is not None:
                assert s + n < UNITS, tile
                out.setdefault(s + n, []).append(tile)
    return out


AHEAD = {"gn": 1, "pq0": 1, "pk0": 1, "pv0": 1, "pq1": 0, "pk1": 0, "pv1": 0}


def tiles_of(post, pre1, pre0, other={}):
    out = []
    for s in range(UNITS):
        for on, at in ((True, other), (post, POST_AT), (pre1, PRE1_AT), (pre0, PRE0_AT)):
            if on:
                out += at.get(s, [])
    return out


def banks():
    bank, last, held = {}, 1, None
    for tile in tiles_of(True, True, True):
        if tile in CLOSES.values():
            held = None
        if tile not in LATER_STEPS:
            last = 1 - last if held is None else 1 - held
            bank[tile] = last
            if tile in CLOSES:
                held = last
    return bank


def claimed(post, pre1, pre0, other={}):
    return [t for t in tiles_of(post, pre1, pre0, other) if t not in LATER_STEPS]


BANK = banks()
LISTS = {"prologue": [t for ts in PRE0_AT.values() for t in ts],
         "first": claimed(False, True, True, FOLD_AT), "steady": claimed(True, True, True),
         "last": claimed(True, True, False), "epilogue": claimed(True, False, False)}
BEFORE = {"first": "prologue", "steady": "steady", "last": "steady", "epilogue": "last"}
BANK[("w1", 0)], BANK[("w1", 1)] = 0, 1
for _first, _last in CLOSES.items():
    BANK[_last] = BANK[_first]
BANK[("fc2", 1)] = BANK[("fc2", 2)] = BANK[("fc2", 0)]


SPARE = 4
EPILOGUE_BANK = {tile: n % (2 + SPARE) for n, tile in enumerate(LISTS["epilogue"])}
for _first, _last in CLOSES.items():
    EPILOGUE_BANK[_last] = EPILOGUE_BANK[_first]
EPILOGUE_BANK[("fc2", 1)] = EPILOGUE_BANK[("fc2", 2)] = EPILOGUE_BANK[("fc2", 0)]


def tile_before(kind, tile):
    here = LISTS[kind]
    number = EPILOGUE_BANK if kind == "epilogue" else BANK
    same = [t for t in here[:here.index(tile)] if number[t] == number[tile]]
    if same:
        return same[-1], 0
    if number[tile] >= 2:
        return None, 0
    if kind == "prologue":
        return None, 0
    return [t for t in LISTS[BEFORE[kind]] if BANK[t] == number[tile]][-1], 1


for _bank in (0, 1):
    _ends = {k: [t for t in LISTS[k] if BANK[t] == _bank][-1] for k in ("prologue", "first", "steady")}
    assert len(set(_ends.values())) == 1, _ends


def build(nc, x, wqkv_t, wproj_t, wqk, fc1_t, fc2_t, params, consts, out):
    with ExitStack() as ctx:
        def sb(name, shape, dt=F32):
            return ctx.enter_context(nc.sbuf_tensor(name, shape, dt))

        def sem(name):
            return ctx.enter_context(nc.semaphore(name))

        x_v = x.rearrange("b (c p) h w -> b p c (h w)", p=P)
        out_v = out.rearrange("b (c p) h w -> b p c (h w)", p=P)

        w_qkv = sb("w_qkv", [P, NC, 3 * C])
        w_proj = sb("w_proj", [P, NC, C])
        w_qk = sb("w_qk", [P, NC, 2 * C])
        w1 = sb("w1", [P, HID])
        w2 = sb("w2", [P, HID // P, LL])
        par = sb("par", [P, PARAM_W])
        con = sb("con", [P, CONST_W])

        xg = sb("xg", [P, NC, L])
        gn_stats = sb("gn_stats", [P, NC, 2, 6])
        gn_mom = sb("gn_mom", [P, NC, 2])
        gn_sq = sb("gn_sq", [P, NC])
        gn_grp = sb("gn_grp", [P, NC, 2])
        gn_var = sb("gn_var", [P, NC])
        gn_rs = sb("gn_rs", [P, NC])
        gn_a = sb("gn_a", [P, NC])
        gn_ma = sb("gn_ma", [P, NC])
        gn_sh = sb("gn_sh", [P, NC])
        hi = sb("hi", [P, L], F32R)
        lo = sb("lo", [P, L], F32R)
        q_st = [sb(f"q_st{g}", [P, HG, L], F32R) for g in range(NG)]
        k_st = sb("k_st", [P, HG, L], F32R)
        v_tok = [sb(f"v_tok{g}", [P, NB, P]) for g in range(NG)]
        v_scaled = sb("v_scaled", [P, 2, P])
        probs = sb("probs", [P, 2, HG, L])
        negmax = sb("negmax", [P, 4])
        sums = sb("sums", [P, 2, HG])
        rsums = sb("rsums", [P, 2, HG])
        att = sb("att", [P, NG, L])
        hi_first, lo_first = (att[:, n, :].bitcast(F32R) for n in range(2))

        x1 = sb("x1", [P, NC, L])
        tok = sb("tok", [P, NB, C])
        ln_ch = sb("ln_ch", [P, NC, L + 2])
        shared = sb("shared", [P, 2 * C // P * L])
        qk_ch = shared[:, 0:2 * L].rearrange("p (g n) -> p g n", g=NG)
        rot_tok = shared[:, 2 * L:4 * L].rearrange("p (r b c) -> p r b c", r=2, b=NB)
        rot_ch = shared[:, 2 * L:4 * L].rearrange("p (a r n) -> p a r n", a=2, r=2)
        hid = shared[:, :].rearrange("p (k m) -> p k m", k=HID // P)
        csum = sb("csum", [P, NB, P])
        lepe_product = csum[:, :, :].rearrange("p b c -> p (b c)")
        par_elu = sb("par_elu", [P, 2, 4])
        t2 = sb("t2", [P, NB, C])
        fc1_nat = t2[:, :, :].rearrange("p (k a) c -> p k (a c)", k=NC)
        elu_e = t2[:, 4:8, :].rearrange("p (a n) c -> p a (n c)", a=2)
        band = sb("band", [P, HALF])
        wait_carrier = sb("wait_carrier", [P, 1])
        ln_st = sb("ln_st", [P, 4, 2, 6])
        ln_mv = sb("ln_mv", [P, 4, 2, 2])
        ln_var = sb("ln_var", [P, 4, 2])
        ln_rs = sb("ln_rs", [P, 4, 2])
        ksum = sb("ksum", [P, 4])
        ksum_g = sb("ksum_g", [P, NG])
        kmean = sb("kmean", [P, NG, HG])
        kv_b = sb("kv_b", [P, NG, D])
        kv_c = sb("kv_c", [P, NG, P])
        kv_s = sb("kv_s", [P, NG, P])
        den = sb("den", [P, NB * NG * HG])
        zden = sb("zden", [P, NB, NG, HG])

        ps_s = [ctx.enter_context(nc.psum_tensor(f"ps_s{n}", [P, L], F32)) for n in range(2)]
        ps_o = ctx.enter_context(nc.psum_tensor("ps_o", [P, L], F32))
        work = [ctx.enter_context(nc.psum_tensor(f"work{n}", [P, HALF], F32)) for n in range(2)]

        epilogue_banks = [work[0][:, :], work[1][:, :]] + [
            ps_s[n // 2][:, HALF * (n % 2):HALF * (n % 2) + HALF] for n in range(SPARE)]
        writing = {"epilogue": False}

        def bank(tile):
            return epilogue_banks[EPILOGUE_BANK[tile]] if writing["epilogue"] else work[BANK[tile]]

        def const(name):
            return con[:, CONSTS[name][0]:CONSTS[name][1]]

        def param(name, n=None):
            a, b = PARAMS[name]
            return par[:, a:b] if n is None else par[:, a + n:a + n + 1]

        early_in = sem("early_in")
        late_in = sem("late_in")
        weights_ready = sem("weights_ready")
        edges_zero = sem("edges_zero")
        x_in = sem("x_in")
        xres_in = sem("xres_in")
        stored = sem("stored")
        gn_step = sem("gn_step")
        gn_math = sem("gn_math")
        gn_done = sem("gn_done")
        hi_done = sem("hi_done")
        lo_done = sem("lo_done")
        q_stacked = sem("q_stacked")
        k_stacked_a = sem("k_stacked_a")
        first_stacked = sem("first_stacked")
        k_stacked_b = sem("k_stacked_b")
        v_done = sem("v_done")
        scores_ready = sem("scores_ready")
        max_ready = sem("max_ready")
        probs_ready = sem("probs_ready")
        rsums_ready = sem("rsums_ready")
        v_scaled_ready = sem("v_scaled_ready")
        pv_done = sem("pv_done")
        att_done = sem("att_done")
        made = {}
        for name in dict.fromkeys(t[0] for k in LISTS.values() for t in k):
            made[name] = sem("made_" + name)
        kv_half = sem("kv_half")
        x1_done = sem("x1_done")
        ln1_step = sem("ln1_step")
        tok_done = sem("tok_done")
        eps_added = sem("eps_added")
        ln1_rsqrt = sem("ln1_rsqrt")
        ln1_done = sem("ln1_done")
        ln_ch_done = sem("ln_ch_done")
        elu_neg_done = sem("elu_neg_done")
        exp_done = sem("exp_done")
        elu_done = sem("elu_done")
        ksum_done = sem("ksum_done")
        kmean_done = sem("kmean_done")
        krot_done = sem("krot_done")
        kvb_done = sem("kvb_done")
        kvc_done = sem("kvc_done")
        kvs_done = sem("kvs_done")
        qrot_done = sem("qrot_done")
        den_done = sem("den_done")
        z_done = sem("z_done")
        attn_done = sem("attn_done")
        u_bias = sem("u_bias")
        lepe_step = sem("lepe_step")
        lepe_pool_step = sem("lepe_pool_step")
        t2_done = sem("t2_done")
        ln2_step = sem("ln2_step")
        ln2_rsqrt = sem("ln2_rsqrt")
        ln2_done = sem("ln2_done")
        r_done = sem("r_done")
        csum_done = sem("csum_done")
        ll_done = sem("ll_done")
        gelu_done = sem("gelu_done")
        band_done = sem("band_done")
        r_ch_done = sem("r_ch_done")
        out_done = sem("out_done")

        EARLY_LOADS, LATE_LOADS = 3 * DMA, 5 * DMA
        POOL_Q, POOL_K = (2, 3), (3,)
        LACK_Q, LACK_K = 4 * len(POOL_Q) * DMA, 4 * len(POOL_K) * DMA
        READ = {
            "w1": (weights_ready, 0, lambda n: 2 + n),
            "gn": (gn_step, 3, lambda n: 3),
            "pq0": (lo_done, 8, lambda n: 1 + n), "pk0": (lo_done, 8, lambda n: 3 + n),
            "pq1": (lo_done, 8, lambda n: 5 + n), "pk1": (lo_done, 8, lambda n: 7 + n),
            "pv0": (v_done, 4, lambda n: 1 + n), "pv1": (v_done, 4, lambda n: 3 + n),
            "proj": (x1_done, 4, lambda n: 1 + n), "x1T": (tok_done, 4, lambda n: 1 + n),
            "lnT": (ln_ch_done, 4, lambda n: 1 + n),
            "k": (elu_done, 8, lambda n: 1 + n), "q": (elu_done, 8, lambda n: 5 + n),
            "kT": (krot_done, 4, lambda n: 1 + n), "kv": (kvc_done, 2, lambda n: 1 + n),
            "kv2": (kvs_done, 2, lambda n: 1 + n), "den": (den_done, 2, lambda n: 1 + n),
            "out": (attn_done, 4, lambda n: 1 + n), "uT": (t2_done, 4, lambda n: 1 + n),
            "ll": (ll_done, 1, lambda n: 1), "fc1": (gelu_done, 8, lambda n: 1 + n),
            "fc2": (band_done, 1, lambda n: 1), "rT": (r_ch_done, 4, lambda n: 1 + n),
            "up": (out_done, 2, lambda n: 1 + n),
        }

        def image_of(i, tile):
            return i + AHEAD.get(tile[0], -1)

        def first_k(b, g):
            return isinstance(b, int) and (b, g) == (0, 0)

        def load_image(eng, b):
            if isinstance(b, int) and b == 0:
                pass
            else:
                eng.wait_ge(made["pk1"], 2 * b)
            eng.dma_start(xg[:, :, :], x_v[b]).then_inc(x_in, DMA)

        def stack_q(eng, b, g, heads=range(HG), on_pool=False):
            eng.wait_ge(lo_done, 8 * b + 4 * g + 2)
            for h in heads:
                for row, part in enumerate((hi, hi, lo, lo)):
                    eng.dma_start(q_st[g][D * row:D * row + D, h, :].bitcast(F32),
                                 part[D * h:D * h + D, :].bitcast(F32))\
                        .then_inc(first_stacked if on_pool else q_stacked, DMA)

        def stack_k(eng, b, g, half, done_units=None, heads=range(HG), on_pool=False):
            hi_k, lo_k = (hi_first, lo_first) if first_k(b, g) else (hi, lo)
            if half == 0:
                eng.wait_ge(lo_done, 8 * b + 4 * g + 4)
            elif done_units is not None:
                eng.wait_ge(scores_ready, done_units)
            cols = slice(half * HALF, half * HALF + HALF)
            signal = first_stacked if on_pool else k_stacked_b if half else k_stacked_a
            for h in heads:
                for row, part in enumerate((hi_k, lo_k, hi_k, lo_k)):
                    eng.dma_start(k_st[D * row:D * row + D, h, cols].bitcast(F32),
                                 part[D * h:D * h + D, cols].bitcast(F32)).then_inc(signal, DMA)

        def rotate_q(eng, b, n):
            g, half = n % 2, n // 2
            cols = slice(half * HALF, half * HALF + HALF)
            if n == 0:
                eng.wait_ge(kv_half, 2 * (b + 1))
            if n >= 2:
                eng.wait_ge(made["out"], 4 * b + n - 1)
            eng.wait_ge(elu_done, 8 * b + 4 + n + 1)
            for r, table in enumerate(("cos_ch", "sin_ch")):
                mu = eng.tensor_tensor(rot_ch[:, n % 2, r, :], qk_ch[:, g, cols], const(table)[:, cols], ALU.mult)
            mu.then_inc(qrot_done, 1)

        def add_norm(eng, b, n):
            rows = slice(2 * n, 2 * n + 2)
            eng.wait_ge(ln2_done, 4 * b + n + 1)
            eng.tensor_tensor(t2[:, rows, :], t2[:, rows, :], tok[:, rows, :], ALU.add).then_inc(r_done, 1)

        block = ctx.enter_context(nc.Block())

        def bodies(eng, prologue, body, epilogue):
            prologue()
            body("first", 0, False, True)
            with eng.Fori(1, B - 1) as i:
                body("steady", i, True, True)
            body("last", B - 1, True, False)
            writing["epilogue"] = True
            epilogue()
            writing["epilogue"] = False

        @block.sync
        def _(sp):
            def load_residual(b):
                if not (isinstance(b, int) and b == 0):
                    sp.wait_ge(stored, NC * DMA * b)
                sp.dma_start(x1[:, :, :], x_v[b]).then_inc(xres_in, DMA)

            def store(b, c):
                sp.wait_ge(out_done, 2 * b + c + 1)
                sp.dma_start(out_v[b][:, c], x1[:, c, :]).then_inc(stored, DMA)

            def prologue():
                for dst, src in ((con[:, 0:EARLY], consts[:, 0:EARLY]), (par[:, :], params),
                                 (w_qkv[:, :, :], wqkv_t)):
                    sp.dma_start(dst, src).then_inc(early_in, DMA)
                for dst, src in ((con[:, EARLY:CONST_W], consts[:, EARLY:CONST_W]), (fc1_nat, fc1_t),
                                 (w_qk[:, :, :], wqk), (w_proj[:, :, :], wproj_t), (w2[:, :, :], fc2_t)):
                    sp.dma_start(dst, src).then_inc(late_in, DMA)
                stack_q(sp, 0, 0, heads=[h for h in range(HG) if h not in POOL_Q])
                stack_k(sp, 0, 0, 0, heads=[h for h in range(HG) if h not in POOL_K])
                stack_k(sp, 0, 0, 1)

            def body(kind, i, post, ahead):
                if kind != "first":
                    stack_k(sp, i, 0, 1, UNITS * i)
                stack_q(sp, i, 1)
                stack_k(sp, i, 1, 0)
                stack_k(sp, i, 1, 1, UNITS * i + PHASE)
                if ahead:
                    stack_q(sp, i + 1, 0)
                    stack_k(sp, i + 1, 0, 0)
                if post:
                    for c in range(NC):
                        store(i - 1, c)
                load_residual(i)

            def epilogue():
                for c in range(NC):
                    store(B - 1, c)
                sp.wait_ge(stored, NC * DMA * B)

            bodies(sp, prologue, body, epilogue)

        @block.tensor
        def _(pe):
            def claim(kind, i, tile):
                before, earlier = tile_before(kind, tile)
                if before is None:
                    return
                signal, per_image, after = READ[before[0]]
                pe.wait_ge(signal, per_image * image_of(i - earlier, before) + after(before[1]))

            def scores(i, s):
                g, j, h = s // PHASE, s % PHASE // HG, s % HG
                if s % PHASE == 0:
                    pe.wait_ge(q_stacked, 16 * DMA * (2 * i + g + 1) - LACK_Q)
                    pe.wait_ge(k_stacked_a, 16 * DMA * (2 * i + g + 1) - LACK_K)
                    if first_k(i, g):
                        pe.wait_ge(first_stacked, LACK_Q + LACK_K)
                if s % PHASE == PHASE // 2:
                    pe.wait_ge(k_stacked_b, 16 * DMA * (2 * i + g + 1))
                if s >= 2 or not (isinstance(i, int) and i == 0):
                    pe.wait_ge(probs_ready, UNITS * i + s - 1)
                for half in range(2):
                    mm = pe.matmul(ps_s[s % 2][:, half * HALF:half * HALF + HALF],
                                   k_st[:, h, j * P:j * P + P],
                                   q_st[g][:, h, half * HALF:half * HALF + HALF], start=True, stop=True)
                mm.then_inc(scores_ready, 1)

            def weigh_values(i, g, j, half):
                n = 2 * NB * i + NB * g + j
                if half == 0:
                    pe.wait_ge(v_scaled_ready, n + 1)
                if j == 0 and not (isinstance(i, int) and i == 0 and g == 0):
                    pe.wait_ge(att_done, 4 * i + 2 * g - 1 + half)
                cols = slice(half * HALF, half * HALF + HALF)
                for h in range(HG):
                    mm = pe.matmul(ps_o[D * h:D * h + D, cols], v_scaled[:, j % 2, D * h:D * h + D],
                                   probs[:, j % 2, h, cols], start=(j == 0), stop=(j == NB - 1))
                mm.then_inc(pv_done, 1)

            def project_heads(kind, i, tile):
                name, half = tile
                g = int(name[2])
                col = (0 if name[1] == "q" else C) + P * g
                b = image_of(i, tile)
                pe.wait_ge(gn_done, NC * (b + 1))
                for c in range(NC):
                    mm = pe.matmul(bank(tile)[:, :], w_qkv[:, c, col:col + P],
                                   xg[:, c, half * HALF:half * HALF + HALF], start=(c == 0), stop=(c == NC - 1))
                mm.then_inc(made[name], 1)

            def project_values(kind, i, tile):
                name, part = tile
                col = 2 * C + P * int(name[2])
                pe.wait_ge(gn_done, NC * (image_of(i, tile) + 1))
                for n in range(4):
                    nb = 4 * part + n
                    for c in range(NC):
                        mm = pe.matmul(bank(tile)[:, P * n:P * n + P], xg[:, c, P * nb:P * nb + P],
                                       w_qkv[:, c, col:col + P], start=(c == 0), stop=(c == NC - 1))
                mm.then_inc(made[name], 1)

            def group_means(kind, i, tile):
                pe.wait_ge(gn_math, 9 * image_of(i, tile) + 2)
                pe.matmul(bank(tile)[:, 0:2 * NC], const("gn_mean"),
                          gn_mom[:, :, :].rearrange("p c t -> p (c t)"), start=True, stop=True)\
                  .then_inc(made["gn"], 1)

            def to_tokens(tile, src):
                for n in range(2):
                    for c in range(NC):
                        nb = 2 * tile[1] + n
                        mm = pe.transpose(bank(tile)[:, C * n + P * c:C * n + P * c + P],
                                          src[:, c, P * nb:P * nb + P], const("ident"))
                mm.then_inc(made[tile[0]], 1)

            def to_channels(tile, src):
                c, half = tile[1] % 2, tile[1] // 2
                for n in range(4):
                    mm = pe.transpose(bank(tile)[:, P * n:P * n + P],
                                      src[:, 4 * half + n, P * c:P * c + P], const("ident"))
                mm.then_inc(made[tile[0]], 1)

            def post_tile(kind, i, tile):
                name, n = tile
                b = image_of(i, tile)
                ps = bank(tile)
                if name == "proj":
                    c, half = n % 2, n // 2
                    pe.wait_ge(att_done, 4 * b + 3 + half)
                    for g in range(NG):
                        mm = pe.matmul(ps[:, :], w_proj[:, g, P * c:P * c + P],
                                       att[:, g, half * HALF:half * HALF + HALF], start=(g == 0), stop=(g == 1))
                    mm.then_inc(made[name], 1)
                elif name == "x1T":
                    pe.wait_ge(x1_done, 4 * b + 2 * (n // 2) + 2)
                    to_tokens(tile, x1)
                elif name == "lnT":
                    pe.wait_ge(ln1_done, 4 * b + 2 * (n // 2) + 2)
                    to_channels(tile, tok)
                elif name in ("k", "q"):
                    g, half = n % 2, n // 2
                    pe.wait_ge(ln_ch_done, 4 * b + 2 * half + 2)
                    col = (C if name == "k" else 0) + P * g
                    for c in range(NC):
                        mm = pe.matmul(ps[:, :], w_qk[:, c, col:col + P],
                                       ln_ch[:, c, 1 + half * HALF:1 + half * HALF + HALF],
                                       start=(c == 0), stop=(c == NC - 1))
                    mm.then_inc(made[name], 1)
                elif name == "kT":
                    g, half = n // 2, n % 2
                    pe.wait_ge(elu_done, 8 * b + 2 * half + g + 1)
                    for t in range(4):
                        nb = 4 * half + t
                        mm = pe.transpose(ps[:, P * t:P * t + P], qk_ch[:, g, P * nb:P * nb + P], const("ident"))
                    mm.then_inc(made[name], 1)
                elif name == "kv":
                    pe.wait_ge(krot_done, 4 * b + 2 * n + 2)
                    for r, at in ((1, D), (0, 0)):
                        for nb in range(NB):
                            for h in range(HG):
                                mm = pe.matmul(ps[D * h:D * h + D, at:at + D],
                                               rot_tok[:, r, nb, D * h:D * h + D],
                                               tok[:, nb, P * n + D * h:P * n + D * h + D],
                                               start=(nb == 0), stop=(r == 1 and nb == NB - 1))
                    mm.then_inc(kv_half, 1)
                elif name == "kv close":
                    pe.wait_ge(kvb_done, 2 * b + n + 1)
                    pe.matmul(ps[:, 0:D], const("rot_t"), kv_b[:, n, :], start=False, stop=True)\
                      .then_inc(made["kv"], 1)
                elif name == "kv2":
                    pe.wait_ge(kvc_done, 2 * b + n + 1)
                    pe.matmul(ps[:, 0:P], const("rot"), kv_c[:, n, :], start=True, stop=True)\
                      .then_inc(made[name], 1)
                elif name == "den":
                    pe.wait_ge(elu_done, 8 * b + 6 + 2 * n)
                    pe.wait_ge(kmean_done, 2 * (b + 1))
                    for t in range(4):
                        nb = 4 * n + t
                        for g in range(NG):
                            at = HG * (NG * t + g)
                            mm = pe.matmul(ps[:, at:at + HG], qk_ch[:, g, P * nb:P * nb + P],
                                           kmean[:, g, :], start=True, stop=True)
                    mm.then_inc(made[name], 1)
                elif name == "out":
                    g, half = n % 2, n // 2
                    pe.wait_ge(qrot_done, 4 * b + n + 1)
                    pe.wait_ge(kvs_done, 2 * b + g + 1)
                    for t in range(4):
                        for r, kv in enumerate((kv_c, kv_s)):
                            mm = pe.matmul(ps[:, P * t:P * t + P], rot_ch[:, n % 2, r, P * t:P * t + P],
                                           kv[:, g, :], start=(r == 0), stop=(r == 1))
                    mm.then_inc(made[name], 1)
                elif name == "uT":
                    pe.wait_ge(lepe_step, 3 * (b + 1))
                    pe.wait_ge(lepe_pool_step, 6 * (b + 1))
                    to_tokens(tile, x1)
                elif name == "ll":
                    pe.wait_ge(csum_done, 4 * (b + 1))
                    for nb in range(NB):
                        mm = pe.matmul(ps[:, 64 * nb:64 * nb + 64], csum[:, nb, :], const("pair_rows"),
                                       start=True, stop=True)
                    mm.then_inc(made[name], 1)
                elif name == "fc1":
                    pe.wait_ge(ll_done, b + 1)
                    pe.matmul(ps[:, :], w1[:, P * n:P * n + P], band[:, :], start=True, stop=True)\
                      .then_inc(made[name], 1)
                elif name == "fc2":
                    pe.wait_ge(gelu_done, 8 * (b + 1))
                    for k in (2 * n, 2 * n + 1):
                        mm = pe.matmul(ps[:, :], w2[:, k, :], hid[:, k, :], start=(k == 0), stop=(k == 7))
                    if n == 3:
                        mm.then_inc(made[name], 1)
                elif name == "rT":
                    pe.wait_ge(r_done, 4 * b + 2 * (n // 2) + 2)
                    to_channels(tile, t2)
                elif name == "up":
                    pe.wait_ge(band_done, b + 1)
                    pe.matmul(ps[:, :], const("spread")[:, P * n:P * n + P], band[:, :], start=True, stop=True)\
                      .then_inc(made[name], 1)

            def post_slot(kind, i, s):
                for tile in POST_AT.get(s, []):
                    if tile not in LATER_STEPS:
                        claim(kind, i, tile)
                    post_tile(kind, i, tile)

            def fold(kind, i, tile):
                claim(kind, i, tile)
                half = tile[1]
                pe.wait_ge(late_in, LATE_LOADS)
                for c in range(NC):
                    mm = pe.matmul(bank(tile)[:, :], const("interp")[:, LL * c:LL * c + LL],
                                   fc1_nat[:, c, half * HALF:half * HALF + HALF],
                                   start=(c == 0), stop=(c == NC - 1))
                mm.then_inc(made["w1"], 1)

            def pre_tile(kind, i, tile):
                claim(kind, i, tile)
                {"g": group_means, "q": project_heads, "k": project_heads,
                 "v": project_values}[tile[0][0 if tile[0] == "gn" else 1]](kind, i, tile)

            def prologue():
                pe.wait_ge(early_in, EARLY_LOADS)
                pe.wait_ge(weights_ready, 1)
                for tiles in PRE0_AT.values():
                    for tile in tiles:
                        pre_tile("prologue", -1, tile)
                scores(0, 0)

            def body(kind, i, post, ahead):
                for s in range(UNITS):
                    if s + 1 < UNITS:
                        scores(i, s + 1)
                    elif ahead:
                        scores(i + 1, 0)
                    if kind == "first":
                        for tile in FOLD_AT.get(s, []):
                            fold(kind, i, tile)
                    if post:
                        post_slot(kind, i, s)
                    for tile in PRE1_AT.get(s, []):
                        pre_tile(kind, i, tile)
                    for tile in PRE0_AT.get(s, []) if ahead else []:
                        pre_tile(kind, i, tile)
                    if s % HG >= 2:
                        n = s // HG - 1
                        if n >= 0:
                            weigh_values(i, n // NB, n % NB, s % HG - 2)
                        elif kind != "first":
                            weigh_values(i - 1, NG - 1, NB - 1, s % HG - 2)

            def epilogue():
                for half in range(2):
                    weigh_values(B - 1, NG - 1, NB - 1, half)
                pe.wait_ge(probs_ready, UNITS * B)
                for s in range(UNITS):
                    post_slot("epilogue", B, s)

            bodies(pe, prologue, body, epilogue)

        @block.scalar
        def _(act):
            def exponentials(i, s):
                j, h = s % PHASE // HG, s % HG
                if s >= 2 * HG or not (isinstance(i, int) and i == 0):
                    act.wait_ge(pv_done, 2 * (2 * NB * i + s // HG - 1))
                act.wait_ge(max_ready, UNITS * i + s + 1)
                act.activation(probs[:, j % 2, h, :], ps_s[s % 2][:, :], ACT.Exp, bias=negmax[:, s % 4:s % 4 + 1],
                               accum_out=sums[:, j % 2, h:h + 1]).then_inc(probs_ready, 1)

            def copy_attention(i, g, half):
                act.wait_ge(pv_done, 2 * (2 * NB * i + NB * (g + 1)) - 1 + half)
                if not (isinstance(i, int) and i == 0):
                    act.wait_ge(made["proj"], 4 * i)
                cols = slice(half * HALF, half * HALF + HALF)
                act.copy(att[:, g, cols], ps_o[:, cols]).then_inc(att_done, 1)

            def gn_apply(b, c):
                act.wait_ge(gn_math, 9 * b + 9)
                act.activation(xg[:, c, :], xg[:, c, :], ACT.Identity, bias=gn_sh[:, c:c + 1],
                               scale=gn_a[:, c:c + 1]).then_inc(gn_done, 1)

            def lepe_bias(b, c):
                act.wait_ge(made["x1T"], 4 * (b + 1))
                act.activation(x1[:, c, :], x1[:, c, :], ACT.Identity, bias=param("lepe_b", c)).then_inc(u_bias, 1)

            def high_part(i, tile):
                name, half = tile
                g, b = int(name[2]), image_of(i, tile)
                is_k = name[1] == "k"
                done = 2 * b + g
                hi_to = hi_first if is_k and first_k(b, g) else hi
                if not (isinstance(done, int) and done == 0):
                    if is_k:
                        act.wait_ge(q_stacked, 16 * DMA * (done + 1) - LACK_Q)
                    else:
                        act.wait_ge(k_stacked_b, 16 * DMA * done)
                act.wait_ge(made[name], 2 * b + half + 1)
                act.activation(hi_to[:, half * HALF:half * HALF + HALF], bank(tile)[:, :], ACT.Identity,
                               bias=param("bk" if is_k else "bq", g)).then_inc(hi_done, 1)

            def post_tile(i, tile):
                name, n = tile
                b = image_of(i, tile)
                ps = bank(tile)
                if name == "x1T":
                    act.wait_ge(made[name], 4 * b + n + 1)
                    act.copy(tok[:, 2 * n:2 * n + 2, :], ps[:, :].rearrange("p (n c) -> p n c", n=2))\
                       .then_inc(tok_done, 1)
                elif name == "kv":
                    act.wait_ge(kv_half, 2 * b + n + 1)
                    act.copy(kv_b[:, n, :], ps[:, D:2 * D]).then_inc(kvb_done, 1)
                elif name == "lnT":
                    c, half = n % 2, n // 2
                    act.wait_ge(made[name], 4 * b + n + 1)
                    act.copy(ln_ch[:, c, 1 + half * HALF:1 + half * HALF + HALF], ps[:, :])\
                       .then_inc(ln_ch_done, 1)
                elif name in ("k", "q"):
                    g = n % 2
                    col = (NG if name == "k" else 0) + g
                    m = (0 if name == "k" else 4) + n
                    if m >= 2:
                        act.wait_ge(elu_done, 8 * b + m - 1)
                    act.wait_ge(made[name], 4 * b + n + 1)
                    act.activation(elu_e[:, m % 2, :], ps[:, :], ACT.Relu, scale=-1.0,
                                   bias=par_elu[:, 0, col:col + 1]).then_inc(elu_neg_done, 1)
                    act.wait_ge(elu_neg_done, 8 * b + m + 1)
                    act.activation(elu_e[:, m % 2, :], elu_e[:, m % 2, :], ACT.Exp, scale=-1.0)\
                       .then_inc(exp_done, 1)
                elif name == "ll":
                    act.wait_ge(made[name], b + 1)
                    act.copy(band[:, :], ps[:, :]).then_inc(ll_done, 1)
                elif name == "fc1":
                    act.wait_ge(made[name], 8 * b + n + 1)
                    act.activation(hid[:, n, :], ps[:, :], ACT.Gelu, bias=param("b1", n)).then_inc(gelu_done, 1)
                elif name == "rT":
                    c, half = n % 2, n // 2
                    act.wait_ge(made[name], 4 * b + n + 1)
                    act.copy(x1[:, c, half * HALF:half * HALF + HALF], ps[:, :]).then_inc(r_ch_done, 1)

            def post_slot(i, s):
                for tile in lagged(POST_AT, ACT_LAG).get(s, []):
                    post_tile(i, tile)
                if s in LEPE_BIAS_AT:
                    lepe_bias(i - 1, LEPE_BIAS_AT[s])

            def pre_slot(i, at, s):
                for tile in lagged(at, ACT_LAG).get(s, []):
                    high_part(i, tile)

            def prologue():
                act.wait_ge(weights_ready, 1)
                for s in range(UNITS):
                    if s in GN_APPLY_AT:
                        gn_apply(0, GN_APPLY_AT[s])
                    pre_slot(-1, PRE0_AT, s)

            def body(kind, i, post, ahead):
                for s in range(UNITS):
                    exponentials(i, s)
                    if s in (3, 4) and kind != "first":
                        copy_attention(i - 1, 1, s - 3)
                    if s in (PHASE + 3, PHASE + 4):
                        copy_attention(i, 0, s - PHASE - 3)
                    if post:
                        post_slot(i, s)
                    pre_slot(i, PRE1_AT, s)
                    if ahead:
                        if s in GN_APPLY_AT:
                            gn_apply(i + 1, GN_APPLY_AT[s])
                        pre_slot(i, PRE0_AT, s)

            def epilogue():
                for half in range(2):
                    copy_attention(B - 1, 1, half)
                for s in range(UNITS):
                    post_slot(B, s)

            bodies(act, prologue, body, epilogue)

        @block.vector
        def _(dve):
            def carry_wait():
                dve.memset(wait_carrier[:, :], 0.0)

            def maximum(i, s):
                dve.wait_ge(scores_ready, UNITS * i + s + 1)
                dve.tensor_reduce(negmax[:, s % 4:s % 4 + 1], ps_s[s % 2][:, :], AX_X, ALU.max, negate=True)\
                   .then_inc(max_ready, 1)

            def invert_sums(i, g, j):
                n = NB * g + j
                dve.wait_ge(probs_ready, UNITS * i + HG * (n + 1))
                dve.reciprocal(rsums[:, j % 2, :], sums[:, j % 2, :]).then_inc(rsums_ready, 1)

            def gn_statistics(b, n):
                c, half = n // 2, n % 2
                dve.wait_ge(x_in, DMA * (b + 1))
                st = dve.bn_stats(gn_stats[:, c, half, :], xg[:, c, half * HALF:half * HALF + HALF])
                if n == 3:
                    st.then_inc(gn_step, 1)

            def gn_moments(b):
                dve.wait_ge(gn_step, 3 * b + 1)
                carry_wait()
                for c in range(NC):
                    ag = dve.bn_aggr(gn_mom[:, c, :], gn_stats[:, c, :, :].rearrange("p a s -> p (a s)"))
                ag.then_inc(gn_step, 1)

            def gn_group(b):
                dve.wait_ge(made["gn"], b + 1)
                dve.tensor_copy(gn_grp[:, :, :].rearrange("p c t -> p (c t)"), bank(("gn", 0))[:, 0:2 * NC])\
                   .then_inc(gn_step, 1)

            def low_part(i, tile):
                name, half = tile
                g, b = int(name[2]), image_of(i, tile)
                is_k = name[1] == "k"
                dve.wait_ge(hi_done, 8 * b + 4 * g + (2 if is_k else 0) + half + 1)
                cols = slice(half * HALF, half * HALF + HALF)
                hi_from, lo_to = (hi_first, lo_first) if is_k and first_k(b, g) else (hi, lo)
                dve.scalar_tensor_tensor(out=lo_to[:, cols], in0=bank(tile)[:, :],
                                         scalar=param("bk" if is_k else "bq", g),
                                         in1=hi_from[:, cols].bitcast(F32), op0=ALU.add, op1=ALU.subtract)\
                   .then_inc(lo_done, 1)

            def values(i, tile):
                name, part = tile
                g, b = int(name[2]), image_of(i, tile)
                if not (isinstance(b, int) and b == 0):
                    dve.wait_ge(v_scaled_ready, 2 * NB * (b - 1) + NB * (g + 1))
                dve.wait_ge(made[name], 2 * b + part + 1)
                bias = param("bv")[:, P * g:P * g + P].rearrange("p (o c) -> p o c", o=1)
                dve.tensor_tensor(v_tok[g][:, 4 * part:4 * part + 4, :],
                                  bank(tile)[:, :].rearrange("p (n c) -> p n c", n=4),
                                  bias.to_broadcast([P, 4, P]), ALU.add).then_inc(v_done, 1)

            def ln_statistics(b, n, src, step):
                for t in range(2):
                    st = dve.bn_stats(ln_st[:, n, t, :], src(t))
                st.then_inc(step, 1)
                dve.wait_ge(step, 8 * b + 2 * n + 1)
                carry_wait()
                for t in range(2):
                    ag = dve.bn_aggr(ln_mv[:, n, t, :], ln_st[:, n, t, :])
                ag.then_inc(step, 1)

            def ln_normalise(b, n, src, rsqrt, done):
                dve.wait_ge(rsqrt, 4 * b + n + 1)
                for t in range(2):
                    nm = dve.tensor_scalar(tok[:, 2 * n + t, :], src(t), ln_mv[:, n, t, 0:1],
                                           ln_rs[:, n, t:t + 1], ALU.subtract, ALU.mult)
                nm.then_inc(done, 1)

            def x1_tokens(n):
                return lambda t: tok[:, 2 * n + t, :]

            def t2_tokens(n):
                return lambda t: t2[:, 2 * n + t, :]

            def four_heads(ap):
                return ap.rearrange("p (n h d) -> p n h d", n=4, h=HG)

            def post_tile(i, tile):
                name, n = tile
                b = image_of(i, tile)
                ps = bank(tile)
                if name == "proj":
                    c, half = n % 2, n // 2
                    cols = slice(half * HALF, half * HALF + HALF)
                    dve.wait_ge(xres_in, DMA * (b + 1))
                    dve.wait_ge(made[name], 4 * b + n + 1)
                    dve.scalar_tensor_tensor(out=x1[:, c, cols], in0=ps[:, :], scalar=param("bproj", c),
                                             in1=x1[:, c, cols], op0=ALU.add, op1=ALU.add).then_inc(x1_done, 1)
                elif name == "x1T":
                    dve.wait_ge(tok_done, 4 * b + n + 1)
                    ln_statistics(b, n, x1_tokens(n), ln1_step)
                elif name in ("k", "q"):
                    elu(b, (0 if name == "k" else 4) + n)
                elif name == "kv close":
                    dve.wait_ge(made["kv"], 2 * b + n + 1)
                    dve.tensor_tensor(kv_c[:, n, :].rearrange("p (h d) -> p h d", h=HG),
                                      ps[:, 0:D].rearrange("p (o d) -> p o d", o=1).to_broadcast([P, HG, D]),
                                      const("head_mask").rearrange("p (h d) -> p h d", h=HG), ALU.mult)\
                       .then_inc(kvc_done, 1)
                elif name == "kT":
                    g, half = n // 2, n % 2
                    if g == 1:
                        dve.wait_ge(kv_half, 2 * b + 1)
                    dve.wait_ge(made[name], 4 * b + n + 1)
                    for r, table in enumerate(("cos_tok", "sin_tok")):
                        tab = const(table)[:, 4 * D * half:4 * D * half + 4 * D]\
                            .rearrange("p (n o d) -> p n o d", n=4, o=1).to_broadcast([P, 4, HG, D])
                        dst = rot_tok[:, r, 4 * half:4 * half + 4, :].rearrange("p n (h d) -> p n h d", h=HG)
                        mu = dve.tensor_tensor(dst, four_heads(ps[:, :]), tab, ALU.mult)
                    mu.then_inc(krot_done, 1)
                elif name == "kv2":
                    dve.wait_ge(made[name], 2 * b + n + 1)
                    dve.tensor_copy(kv_s[:, n, :], ps[:, 0:P]).then_inc(kvs_done, 1)
                elif name == "den":
                    dve.wait_ge(made[name], 2 * b + n + 1)
                    width = 4 * NG * HG
                    dve.tensor_scalar(den[:, width * n:width * n + width], ps[:, 0:width], 1e-6, None, ALU.add)\
                       .then_inc(den_done, 1)
                    dve.wait_ge(den_done, 2 * b + n + 1)
                    dve.reciprocal(zden[:, 4 * n:4 * n + 4, :, :].rearrange("p n g h -> p (n g h)"),
                                   den[:, width * n:width * n + width]).then_inc(z_done, 1)
                elif name == "out":
                    g, half = n % 2, n // 2
                    dve.wait_ge(z_done, 2 * b + half + 1)
                    dve.wait_ge(made[name], 4 * b + n + 1)
                    z = zden[:, 4 * half:4 * half + 4, g, :].rearrange("p n (h o) -> p n h o", o=1)
                    dst = t2[:, 4 * half:4 * half + 4, P * g:P * g + P].rearrange("p n (h d) -> p n h d", h=HG)
                    dve.tensor_tensor(dst, four_heads(ps[:, :]), z.to_broadcast([P, 4, HG, D]), ALU.mult)\
                       .then_inc(attn_done, 1)
                elif name == "uT":
                    dve.wait_ge(attn_done, 4 * b + 2 * (n // 2) + 2)
                    dve.wait_ge(made[name], 4 * b + n + 1)
                    both = t2[:, 2 * n:2 * n + 2, :]
                    dve.tensor_tensor(both, ps[:, :].rearrange("p (n c) -> p n c", n=2), both, ALU.add)\
                       .then_inc(t2_done, 1)
                    dve.wait_ge(t2_done, 4 * b + n + 1)
                    ln_statistics(b, n, t2_tokens(n), ln2_step)
                elif (name, n) == ("fc2", 3):
                    dve.wait_ge(made[name], b + 1)
                    dve.scalar_tensor_tensor(out=band[:, :], in0=ps[:, :], scalar=param("b2"), in1=band[:, :],
                                             op0=ALU.add, op1=ALU.subtract).then_inc(band_done, 1)
                elif name == "up":
                    dve.wait_ge(r_ch_done, 4 * (b + 1))
                    dve.wait_ge(made[name], 2 * b + n + 1)
                    pairs = x1[:, n, :].rearrange("p (m t) -> p m t", t=2)
                    up = ps[:, :].rearrange("p (m o) -> p m o", o=1).to_broadcast([P, HALF, 2])
                    dve.tensor_tensor(pairs, up, pairs, ALU.add).then_inc(out_done, 1)

            def elu(b, m):
                is_q, n = m // 4, m % 4
                g, half = n % 2, n // 2
                if is_q:
                    dve.wait_ge(made["kT"], 4 * b + 2 * g + half + 1)
                dve.wait_ge(exp_done, 8 * b + m + 1)
                col = (0 if is_q else NG) + g
                dve.scalar_tensor_tensor(out=qk_ch[:, g, half * HALF:half * HALF + HALF],
                                         in0=bank(("q" if is_q else "k", n))[:, :],
                                         scalar=par_elu[:, 1, col:col + 1], in1=elu_e[:, m % 2, :],
                                         op0=ALU.add, op1=ALU.max,
                                         accum_out=None if is_q else ksum[:, n:n + 1]).then_inc(elu_done, 1)

            def lepe(b, c, tap):
                signal, each = ((lepe_step, 1), (lepe_pool_step, 2))[c]
                if tap == 0:
                    dve.wait_ge(edges_zero, 2)
                    dve.wait_ge(ln_ch_done, 4 * (b + 1))
                    dve.wait_ge(u_bias, 2 * b + c + 1)
                else:
                    dve.wait_ge(signal, each * (3 * b + tap))
                dve.scalar_tensor_tensor(out=x1[:, c, :], in0=ln_ch[:, c, tap:tap + L],
                                         scalar=param("lepe_w", 3 * c + tap), in1=x1[:, c, :],
                                         op0=ALU.mult, op1=ALU.add).then_inc(signal, each)

            def post_slot(kind, i, s):
                b = i - 1
                for name, n in lagged(POST_AT, DVE_NORM_LAG).get(s, []):
                    if name == "x1T":
                        ln_normalise(b, n, x1_tokens(n), ln1_rsqrt, ln1_done)
                    else:
                        ln_normalise(b, n, t2_tokens(n), ln2_rsqrt, ln2_done)
                        if kind == "epilogue":
                            add_norm(dve, b, n)
                for tile in lagged(POST_AT, DVE_LAG).get(s, []):
                    post_tile(i, tile)
                if s in LEPE_DVE_AT:
                    for c in range(NC if kind == "epilogue" else 1):
                        lepe(b, c, LEPE_DVE_AT[s])
                if kind == "epilogue" and s in ROTATE_AT:
                    rotate_q(dve, b, ROTATE_AT[s])

            def pre_slot(i, at, s):
                for tile in lagged(at, DVE_LAG).get(s, []):
                    if tile[0] == "gn":
                        gn_group(image_of(i, tile))
                    elif tile[0][1] in "qk":
                        low_part(i, tile)
                    else:
                        values(i, tile)

            def prologue():
                for n in range(4):
                    gn_statistics(0, n)
                gn_moments(0)
                dve.wait_ge(early_in, EARLY_LOADS)
                for c in range(NC):
                    dve.tensor_scalar(w_qkv[:, c, 0:C], w_qkv[:, c, 0:C], float(D) ** -0.5, None, ALU.mult)
                dve.tensor_scalar(param("bq"), param("bq"), float(D) ** -0.5, None, ALU.mult).then_inc(weights_ready, 1)
                dve.tensor_scalar(par_elu[:, 0, :], param("bqk"), -1.0, None, ALU.mult)
                dve.tensor_scalar(par_elu[:, 1, :], param("bqk"), 1.0, None, ALU.add)
                for s in range(UNITS):
                    pre_slot(-1, PRE0_AT, s)

            def body(kind, i, post, ahead):
                for s in range(UNITS):
                    maximum(i, s)
                    if s % HG == 0:
                        n = s // HG - 1
                        if n >= 0:
                            invert_sums(i, n // NB, n % NB)
                        elif kind != "first":
                            invert_sums(i - 1, NG - 1, NB - 1)
                    if kind == "first" and s - 2 in FOLD_AT:
                        half = FOLD_AT[s - 2][0][1]
                        dve.wait_ge(made["w1"], half + 1)
                        dve.tensor_copy(w1[:, half * HALF:half * HALF + HALF], work[half][:, :])\
                           .then_inc(weights_ready, 1)
                    if post:
                        post_slot(kind, i, s)
                    pre_slot(i, PRE1_AT, s)
                    if ahead:
                        for n in GN_STATS_AT.get(s, []):
                            gn_statistics(i + 1, n)
                        if s == GN_MOMENTS_AT:
                            gn_moments(i + 1)
                        pre_slot(i, PRE0_AT, s)

            def epilogue():
                invert_sums(B - 1, NG - 1, NB - 1)
                for s in range(UNITS):
                    post_slot("epilogue", B, s)

            bodies(dve, prologue, body, epilogue)

        @block.gpsimd
        def _(pool):
            def scale_values(i, g, j):
                n = 2 * NB * i + NB * g + j
                pool.wait_ge(v_done, 4 * i + 2 * g + 2)
                if j >= 2 or not (isinstance(i, int) and i == 0 and g == 0):
                    pool.wait_ge(pv_done, 2 * (n - 1))
                pool.wait_ge(rsums_ready, n + 1)
                r = rsums[:, j % 2, :].rearrange("p (h o) -> p h o", o=1)
                pool.tensor_tensor(v_scaled[:, j % 2, :].rearrange("p (h d) -> p h d", h=HG),
                                   v_tok[g][:, j, :].rearrange("p (h d) -> p h d", h=HG),
                                   r.to_broadcast([P, HG, D]), ALU.mult).then_inc(v_scaled_ready, 1)

            def gn_step_of(b, n, out, in0, in1, op):
                if n > 0:
                    pool.wait_ge(gn_math, 9 * b + n)
                pool.tensor_tensor(out, in0, in1, op).then_inc(gn_math, 1)

            def gn_mean_squares(b):
                pool.wait_ge(gn_step, 3 * b + 2)
                gn_step_of(b, 0, gn_sq[:, :], gn_mom[:, :, 0], gn_mom[:, :, 0], ALU.mult)
                gn_step_of(b, 1, gn_mom[:, :, 1], gn_mom[:, :, 1], gn_sq[:, :], ALU.add)

            def gn_affine(b):
                mean, square = gn_grp[:, :, 0], gn_grp[:, :, 1]
                pool.wait_ge(gn_step, 3 * b + 3)
                gn_step_of(b, 2, gn_sq[:, :], mean, mean, ALU.mult)
                gn_step_of(b, 3, gn_var[:, :], square, gn_sq[:, :], ALU.subtract)
                gn_step_of(b, 4, gn_var[:, :], gn_var[:, :], const("eps"), ALU.add)
                gn_step_of(b, 5, gn_rs[:, :], gn_var[:, :], const("minus_half")[:, 0:NC], ALU.pow)
                gn_step_of(b, 6, gn_a[:, :], gn_rs[:, :], param("gn_w"), ALU.mult)
                gn_step_of(b, 7, gn_ma[:, :], mean, gn_a[:, :], ALU.mult)
                gn_step_of(b, 8, gn_sh[:, :], param("gn_b"), gn_ma[:, :], ALU.subtract)

            def rsqrt(step, b, n, done):
                pool.wait_ge(step, 8 * b + 2 * n + 2)
                pool.tensor_tensor(ln_var[:, n, :], ln_mv[:, n, :, 1], const("eps"), ALU.add).then_inc(eps_added, 1)
                pool.wait_ge(eps_added, 8 * b + (4 if step is ln2_step else 0) + n + 1)
                pool.tensor_tensor(ln_rs[:, n, :], ln_var[:, n, :], const("minus_half")[:, 0:2], ALU.pow)\
                    .then_inc(done, 1)

            def lepe(b, m):
                tap = m // 2
                if m == 0:
                    pool.wait_ge(ln_ch_done, 4 * (b + 1))
                    pool.wait_ge(u_bias, 2 * b + 2)
                else:
                    pool.wait_ge(lepe_pool_step, 6 * b + m)
                if m % 2 == 0:
                    pool.tensor_tensor(lepe_product, ln_ch[:, 1, tap:tap + L],
                                       param("lepe_w", 3 + tap).to_broadcast([P, L]), ALU.mult)\
                        .then_inc(lepe_pool_step, 1)
                else:
                    pool.tensor_tensor(x1[:, 1, :], x1[:, 1, :], lepe_product, ALU.add)\
                        .then_inc(lepe_pool_step, 1)

            def pair_sums(b, n):
                rows = slice(2 * n, 2 * n + 2)
                pool.wait_ge(ln2_done, 4 * b + n + 1)
                pool.tensor_tensor(csum[:, rows, :], tok[:, rows, 0:C:2], tok[:, rows, 1:C:2], ALU.add)\
                    .then_inc(csum_done, 1)

            def post_slot(kind, i, s):
                b = i - 1
                steady = kind != "epilogue"
                for name, n in lagged(POST_AT, POOL_LAG).get(s, []):
                    if name == "x1T":
                        rsqrt(ln1_step, b, n, ln1_rsqrt)
                    else:
                        rsqrt(ln2_step, b, n, ln2_rsqrt)
                if s == KMEAN_AT:
                    pool.wait_ge(elu_done, 8 * b + 4)
                    pool.tensor_tensor(ksum_g[:, :], ksum[:, 0:2], ksum[:, 2:4], ALU.add).then_inc(ksum_done, 1)
                    pool.wait_ge(ksum_done, b + 1)
                    for g in range(NG):
                        pool.tensor_tensor(kmean[:, g, :], const("head_mean"),
                                           ksum_g[:, g:g + 1].to_broadcast([P, HG]), ALU.mult)\
                            .then_inc(kmean_done, 1)
                if steady and s in LEPE_POOL_AT:
                    lepe(b, LEPE_POOL_AT[s])
                if steady and s in ROTATE_AT:
                    rotate_q(pool, b, ROTATE_AT[s])
                for _, n in lagged(POST_AT, POOL_SUM_LAG).get(s, []):
                    pair_sums(b, n)
                    if steady:
                        add_norm(pool, b, n)

            def prologue():
                load_image(pool, 0)
                for col in (0, L + 1):
                    pool.memset(ln_ch[:, :, col:col + 1], 0.0).then_inc(edges_zero, 1)
                pool.wait_ge(early_in, EARLY_LOADS)
                gn_mean_squares(0)
                gn_affine(0)
                stack_q(pool, 0, 0, heads=POOL_Q, on_pool=True)
                stack_k(pool, 0, 0, 0, heads=POOL_K, on_pool=True)

            def body(kind, i, post, ahead):
                for s in range(UNITS):
                    if s % HG == 1:
                        n = s // HG - 1
                        if n >= 0:
                            scale_values(i, n // NB, n % NB)
                        elif kind != "first":
                            scale_values(i - 1, NG - 1, NB - 1)
                    if post:
                        post_slot(kind, i, s)
                    if ahead:
                        if s == LOAD_AT:
                            load_image(pool, i + 1)
                        if s == GN_MOMENTS_AT:
                            gn_mean_squares(i + 1)
                        if s in lagged(PRE0_AT, POOL_LAG):
                            gn_affine(i + 1)

            def epilogue():
                scale_values(B - 1, NG - 1, NB - 1)
                for s in range(UNITS):
                    post_slot("epilogue", B, s)

            bodies(pool, prologue, body, epilogue)


def constants():
    p = np.arange(P)
    con = {n: np.zeros((P, b - a), np.float32) for n, (a, b) in CONSTS.items()}
    con["ident"][p, p] = 1
    con["gn_mean"][:] = (p[:, None] // GN_SIZE == p[None, :] // GN_SIZE) / GN_SIZE
    rot = np.zeros((P, P), np.float32)
    low = p % D < D // 2
    rot[p[low], p[low] + D // 2] = -1
    rot[p[~low], p[~low] - D // 2] = 1
    con["rot"][:] = rot
    con["rot_t"][:] = rot.T
    con["head_mask"][:] = (p[:, None] // D == p[None, :] // D) / L
    con["head_mean"][:] = (p[:, None] // D == np.arange(HG)[None, :]) / L
    con["pair_rows"][:] = 0.5 * (p[:, None] // 2 == np.arange(P // 2)[None, :])
    con["spread"][:] = 0.5 * (p[:, None] == np.arange(C)[None, :] // 2)
    pos = np.linspace(0.0, 1.0, C, dtype=np.float32) * np.float32(LL - 1)
    i0 = np.clip(np.floor(pos).astype(np.int32), 0, LL - 2)
    w = pos - i0.astype(np.float32)
    interp = np.zeros((C, LL), np.float32)
    interp[np.arange(C), i0] = np.float32(1.0) - w
    interp[np.arange(C), i0 + 1] = w
    con["interp"][:] = interp.reshape(NC, P, LL).transpose(1, 0, 2).reshape(P, NC * LL)
    con["minus_half"][:] = -0.5
    con["eps"][:] = 1e-5
    inv_freq = (1.0 / np.float32(10000.0) ** (np.arange(0, D, 2, dtype=np.float32) / np.float32(D))).astype(np.float32)
    freqs = np.outer(np.arange(L, dtype=np.float32), inv_freq).astype(np.float32)
    emb = np.concatenate([freqs, freqs], axis=-1)
    for name, table in (("cos", np.cos(emb)), ("sin", np.sin(emb))):
        con[name + "_tok"][:] = table.reshape(NB, P, D).transpose(1, 0, 2).reshape(P, NB * D)
        con[name + "_ch"][:] = np.tile(table.T, (HG, 1))
    return np.ascontiguousarray(np.concatenate([con[n] for n in CONSTS], axis=1))


def kernel(x, L0_conv_gn_w, L0_conv_gn_b, L0_conv_w_qkv, L0_conv_b_qkv, L0_conv_w_proj, L0_conv_b_proj,
           L1_attn_Wqk, L1_attn_bqk, L1_attn_lepe_w, L1_attn_lepe_b, L1_ffn_fc1_w, L1_ffn_fc1_b,
           L1_ffn_fc2_w, L1_ffn_fc2_b):
    import concourse.bacc as bacc
    from concourse.bass_utils import run_bass_kernel_spmd

    def halves(a):
        a = np.asarray(a)
        return np.ascontiguousarray(a.reshape(-1, P, a.shape[-1]).transpose(1, 0, 2))

    def columns(a):
        return np.asarray(a).reshape(-1, P).T

    heads = C // D
    w_qkv = np.asarray(L0_conv_w_qkv).reshape(heads, 3, D, C).transpose(1, 0, 2, 3).reshape(3 * C, C)
    b_qkv = np.asarray(L0_conv_b_qkv).reshape(heads, 3, D).transpose(1, 0, 2).reshape(3, C)
    lepe_w = np.asarray(L1_attn_lepe_w).reshape(NC, P, 3).transpose(1, 0, 2).reshape(P, NC * 3)
    par = {"bq": columns(b_qkv[0]), "bk": columns(b_qkv[1]), "bproj": columns(L0_conv_b_proj),
           "bqk": columns(L1_attn_bqk), "lepe_w": lepe_w, "lepe_b": columns(L1_attn_lepe_b),
           "b1": columns(L1_ffn_fc1_b), "b2": columns(L1_ffn_fc2_b), "gn_w": columns(L0_conv_gn_w),
           "gn_b": columns(L0_conv_gn_b), "bv": np.broadcast_to(b_qkv[2][None, :], (P, C))}
    arrays = {
        "x": np.ascontiguousarray(x),
        "wqkv_t": halves(w_qkv.T), "wproj_t": halves(np.asarray(L0_conv_w_proj).T), "wqk": halves(L1_attn_Wqk),
        "fc1_t": halves(np.asarray(L1_ffn_fc1_w).T), "fc2_t": halves(np.asarray(L1_ffn_fc2_w).T),
        "params": np.ascontiguousarray(np.concatenate([par[n] for n in PARAMS], axis=1)),
        "consts": constants(),
    }
    nc = bacc.Bacc("TRN2", target_bir_lowering=False, num_devices=1)
    args = [nc.dram_tensor("in_" + n, a.shape, mybir.dt.from_np(a.dtype), kind="ExternalInput").ap()
            for n, a in arrays.items()]
    args.append(nc.dram_tensor("out_x", (B, C, 32, 32), F32, kind="ExternalOutput").ap())
    build(nc, *args)
    r = run_bass_kernel_spmd(nc, [{"in_" + n: a for n, a in arrays.items()}], core_ids=[0])
    return r.results[0]["out_x"]
```
